# Optimizing a Trainium2 kernel written in Bass

```python
import numpy as np
import jax
import jax.numpy as jnp

def _softmax(x, axis=-1):
    return jax.nn.softmax(x, axis=axis)

def _gelu(x):
    return jax.nn.gelu(x, approximate=True)

def _silu(x):
    return jax.nn.silu(x)

def _sigmoid(x):
    return jax.nn.sigmoid(x)

def _layernorm(x, axis=-1, eps=1e-05):
    m = jnp.mean(x, axis=axis, keepdims=True)
    v = jnp.var(x, axis=axis, keepdims=True)
    return (x - m) / jnp.sqrt(v + eps)

def _scatter_add(tgt, idx, src, axis=0):
    return tgt.at[idx].add(src)

def _segment_sum(src, seg, n):
    return jax.ops.segment_sum(src, seg, n)
kernel_name = 'mk_xattn_seq_d2_seqx_r4_f62b4f'

def setup_inputs(seed: int=0):
    np.random.seed(seed)
    _w = jnp.asarray

    def _rec_inputs():
        import jax
        import jax.numpy as jnp
        _rk = jax.random.key(seed)
        x = -0.0002928 + 1 * jax.random.normal(jax.random.fold_in(_rk, 1), (8, 256, 512), jnp.float32)
        _lenS = 256 - jax.random.randint(jax.random.fold_in(_rk, 7), (8,), 0, max(1, 256 // 4) + 1, jnp.int32)
        _lenS2 = 256 - jax.random.randint(jax.random.fold_in(_rk, 8), (8,), 0, max(1, 256 // 4) + 1, jnp.int32)
        _ctx_2048P = jax.random.normal(jax.random.fold_in(_rk, 11), (8, 16, 512), jnp.float32)
        _ctx_2048c = jax.random.dirichlet(jax.random.fold_in(_rk, 511), 0.3 * jnp.ones((16,), jnp.float32), (8, 256))
        _ctx_2048t = jnp.einsum('bsk,bkd->bsd', _ctx_2048c, _ctx_2048P)
        _ctx_2048t = _ctx_2048t * jax.lax.rsqrt(jnp.mean(jnp.square(_ctx_2048t)) + 1e-12) * 0.953939
        ctx_2048 = -1.39393e-06 + 0.999914 * (_ctx_2048t + 0.3 * jax.random.normal(jax.random.fold_in(_rk, 611), (8, 256, 512), jnp.float32))
        _validS = jnp.arange(256)[None, :] < _lenS[:, None]
        _validS2 = jnp.arange(256)[None, :] < _lenS2[:, None]
        _causal = jnp.tril(jnp.ones((256, 256), dtype=bool))
        mask_1x1xSxS2_fc1 = jnp.where(jnp.broadcast_to(_validS2[0:1, None, None, :], (1, 1, 256, 256)), 1.0, 0.0).astype(jnp.float32)
        mask_Bx1xSxS2_ff1 = jnp.where(jnp.ones((8, 1, 256, 256), dtype=bool), 1.0, 0.0).astype(jnp.float32)
        return (x, ctx_2048, mask_1x1xSxS2_fc1, mask_Bx1xSxS2_ff1)
    x, ctx_2048, mask_1x1xSxS2_fc1, mask_Bx1xSxS2_ff1 = _rec_inputs()

    def _L0_xattn_setup():
        import jax, jax.numpy as jnp
        import numpy as np
        H = 512
        NH = 16
        HD = H // NH
        EPS = 1e-05

        def gelu(x):
            return 0.5 * x * (1.0 + jnp.tanh(0.7978845608028654 * x * (1.0 + 0.044715 * x * x)))

        def layernorm(x, scale, bias):
            m = jnp.mean(x, axis=-1, keepdims=True)
            v = jnp.mean(jnp.square(x - m), axis=-1, keepdims=True)
            return (x - m) * jax.lax.rsqrt(v + EPS) * scale + bias

        def split_heads(x):
            b, s, _ = x.shape
            return x.reshape(b, s, NH, HD).transpose(0, 2, 1, 3)

        def merge_heads(x):
            b, nh, s, hd = x.shape
            return x.transpose(0, 2, 1, 3).reshape(b, s, nh * hd)

        def attention(q, k, v, mask):
            scores = jnp.einsum('bhqd,bhkd->bhqk', q, k) / jnp.sqrt(jnp.float32(HD))
            scores = scores * mask - 10000.0 * (1.0 - mask)
            probs = jax.nn.softmax(scores, axis=-1)
            return jnp.einsum('bhqk,bhkd->bhqd', probs, v)
        key = jax.random.key(seed)
        ks = jax.random.split(key, 16)
        b, s, t = (2, 256, 256)
        w = lambda k, i, o: jax.random.normal(k, (i, o), jnp.float32) * 0.02
        inp = {'hidden_states': jax.random.normal(ks[0], (b, s, H), jnp.float32), 'encoder_states': jax.random.normal(ks[1], (b, t, H), jnp.float32), 'ltor_mask': jnp.tril(jnp.ones((1, 1, s, s), jnp.float32)), 'cross_mask': jnp.ones((b, 1, s, t), jnp.float32), 'ln1_s': jnp.ones((H,), jnp.float32), 'ln1_b': jnp.zeros((H,), jnp.float32), 'w_qkv': w(ks[2], H, 3 * H), 'b_qkv': jnp.zeros((3 * H,), jnp.float32), 'w_ao': w(ks[3], H, H), 'b_ao': jnp.zeros((H,), jnp.float32), 'ln2_s': jnp.ones((H,), jnp.float32), 'ln2_b': jnp.zeros((H,), jnp.float32), 'w_q': w(ks[4], H, H), 'b_q': jnp.zeros((H,), jnp.float32), 'w_kv': w(ks[5], H, 2 * H), 'b_kv': jnp.zeros((2 * H,), jnp.float32), 'w_co': w(ks[6], H, H), 'b_co': jnp.zeros((H,), jnp.float32), 'ln3_s': jnp.ones((H,), jnp.float32), 'ln3_b': jnp.zeros((H,), jnp.float32), 'w1': w(ks[7], H, 4 * H), 'b1': jnp.zeros((4 * H,), jnp.float32), 'w2': w(ks[8], 4 * H, H), 'b2': jnp.zeros((H,), jnp.float32)}
        return inp
    _L0_xattn_all = _L0_xattn_setup()
    _L0_xattn_in = {k: v for k, v in _L0_xattn_all.items() if k in ('ln1_s', 'ln1_b', 'w_qkv', 'b_qkv', 'w_ao', 'b_ao', 'ln2_s', 'ln2_b', 'w_q', 'b_q', 'w_kv', 'b_kv', 'w_co', 'b_co', 'ln3_s', 'ln3_b', 'w1', 'b1', 'w2', 'b2')}
    del _L0_xattn_all

    def _L1_xattn_setup():
        import jax, jax.numpy as jnp
        import numpy as np
        E, H, L, B = (512, 32, 256, 4)
        S = E // H
        DM, DD = (32, 64)

        def _ln(x, w, b, eps=1e-05):
            m = x.mean(-1, keepdims=True)
            v = ((x - m) ** 2).mean(-1, keepdims=True)
            return (x - m) / jnp.sqrt(v + eps) * w + b

        def _block(x, state, ln1_w, ln1_b, ln2_w, ln2_b, maa_x, maa_w1, maa_w2, maa_stack, time_decay, td_w1, td_w2, u, Wr, Wk, Wv, Wg, Wo, gn_w, gn_b, ffn_maa_k, ffn_maa_r, Wfk, Wfr, Wfv):
            b, l, e = x.shape
            h = u.shape[0]
            s_ = e // h
            xa = _ln(x, ln1_w, ln1_b)
            sx = jnp.concatenate([state[:, 1:2] - xa[:, :1], xa[:, :-1] - xa[:, 1:]], axis=1)
            xxx = jnp.tanh((xa + sx * maa_x) @ maa_w1).reshape(b, l, 5, DM)
            xxx = jnp.einsum('blfd,fde->blfe', xxx, maa_w2)
            xm = xa[:, :, None] + sx[:, :, None] * (maa_stack + xxx)
            xk, xw, xv, xr, xg = (xm[:, :, j] for j in range(5))
            w = jnp.exp(-jnp.exp(time_decay + jnp.tanh(xw @ td_w1) @ td_w2)).reshape(b, l, h, s_)
            r = (xr @ Wr.T).reshape(b, l, h, s_)
            k = (xk @ Wk.T).reshape(b, l, h, s_)
            v = (xv @ Wv.T).reshape(b, l, h, s_)
            g = jax.nn.silu(xg @ Wg.T)
            s0 = state[:, 2:2 + s_].reshape(b, h, s_, s_)

            def step(s, rkvw):
                r_t, k_t, v_t, w_t = rkvw
                a = k_t[..., :, None] * v_t[..., None, :]
                out = jnp.einsum('bhi,bhij->bhj', r_t, u * a + s)
                s = a + w_t[..., :, None] * s
                return (s, out)
            rkvw = tuple((jnp.moveaxis(t, 1, 0) for t in (r, k, v, w)))
            _, out = jax.lax.scan(step, s0, rkvw)
            out = jnp.moveaxis(out, 0, 1).reshape(b, l, e)
            og = out.reshape(b, l, h, s_)
            m = og.mean(-1, keepdims=True)
            va = ((og - m) ** 2).mean(-1, keepdims=True)
            og = ((og - m) / jnp.sqrt(va + 1e-05)).reshape(b, l, e) * gn_w + gn_b
            x1 = x + og * g @ Wo.T
            xc = _ln(x1, ln2_w, ln2_b)
            sx2 = jnp.concatenate([state[:, 0:1] - xc[:, :1], xc[:, :-1] - xc[:, 1:]], axis=1)
            xk2 = xc + sx2 * ffn_maa_k
            xr2 = xc + sx2 * ffn_maa_r
            rr = jax.nn.sigmoid(xr2 @ Wfr.T)
            kk = jnp.square(jax.nn.relu(xk2 @ Wfk.T))
            return x1 + rr * (kk @ Wfv.T)
        key = jax.random.key(seed)
        ks = jax.random.split(key, 24)
        sc = 0.02
        d = {'x': jax.random.normal(ks[0], (B, L, E), jnp.float32), 'state': jax.random.normal(ks[1], (B, 2 + S, E), jnp.float32) * 0.1, 'ln1_w': jnp.ones((E,), jnp.float32), 'ln1_b': jnp.zeros((E,), jnp.float32), 'ln2_w': jnp.ones((E,), jnp.float32), 'ln2_b': jnp.zeros((E,), jnp.float32), 'maa_x': jax.random.normal(ks[2], (E,), jnp.float32) * 0.1, 'maa_w1': jax.random.normal(ks[3], (E, 5 * DM), jnp.float32) * sc, 'maa_w2': jax.random.normal(ks[4], (5, DM, E), jnp.float32) * sc, 'maa_stack': jax.random.normal(ks[5], (1, 5, E), jnp.float32) * 0.1, 'time_decay': jax.random.normal(ks[6], (E,), jnp.float32) * 0.5, 'td_w1': jax.random.normal(ks[7], (E, DD), jnp.float32) * sc, 'td_w2': jax.random.normal(ks[8], (DD, E), jnp.float32) * sc, 'u': jax.random.normal(ks[9], (H, S, 1), jnp.float32) * 0.1, 'Wr': jax.random.normal(ks[10], (E, E), jnp.float32) * sc, 'Wk': jax.random.normal(ks[11], (E, E), jnp.float32) * sc, 'Wv': jax.random.normal(ks[12], (E, E), jnp.float32) * sc, 'Wg': jax.random.normal(ks[13], (E, E), jnp.float32) * sc, 'Wo': jax.random.normal(ks[14], (E, E), jnp.float32) * sc, 'gn_w': jnp.ones((E,), jnp.float32), 'gn_b': jnp.zeros((E,), jnp.float32), 'ffn_maa_k': jax.random.normal(ks[15], (E,), jnp.float32) * 0.1, 'ffn_maa_r': jax.random.normal(ks[16], (E,), jnp.float32) * 0.1, 'Wfk': jax.random.normal(ks[17], (E, E), jnp.float32) * sc, 'Wfr': jax.random.normal(ks[18], (E, E), jnp.float32) * sc, 'Wfv': jax.random.normal(ks[19], (E, E), jnp.float32) * sc}
        return d
    _L1_xattn_all = _L1_xattn_setup()
    _L1_xattn_in = {k: v for k, v in _L1_xattn_all.items() if k in ('ln1_w', 'ln1_b', 'ln2_w', 'ln2_b', 'maa_x', 'maa_w1', 'maa_w2', 'maa_stack', 'time_decay', 'td_w1', 'td_w2', 'u', 'Wr', 'Wk', 'Wv', 'Wg', 'Wo', 'gn_w', 'gn_b', 'ffn_maa_k', 'ffn_maa_r', 'Wfk', 'Wfr', 'Wfv')}
    del _L1_xattn_all
    return {'x': x, 'ctx_2048': ctx_2048, 'mask_1x1xSxS2_fc1': mask_1x1xSxS2_fc1, 'mask_Bx1xSxS2_ff1': mask_Bx1xSxS2_ff1, 'L0_xattn_ln1_s': _L0_xattn_in['ln1_s'], 'L0_xattn_ln1_b': _L0_xattn_in['ln1_b'], 'L0_xattn_w_qkv': _L0_xattn_in['w_qkv'], 'L0_xattn_b_qkv': _L0_xattn_in['b_qkv'], 'L0_xattn_w_ao': _L0_xattn_in['w_ao'], 'L0_xattn_b_ao': _L0_xattn_in['b_ao'], 'L0_xattn_ln2_s': _L0_xattn_in['ln2_s'], 'L0_xattn_ln2_b': _L0_xattn_in['ln2_b'], 'L0_xattn_w_q': _L0_xattn_in['w_q'], 'L0_xattn_b_q': _L0_xattn_in['b_q'], 'L0_xattn_w_kv': _L0_xattn_in['w_kv'], 'L0_xattn_b_kv': _L0_xattn_in['b_kv'], 'L0_xattn_w_co': _L0_xattn_in['w_co'], 'L0_xattn_b_co': _L0_xattn_in['b_co'], 'L0_xattn_ln3_s': _L0_xattn_in['ln3_s'], 'L0_xattn_ln3_b': _L0_xattn_in['ln3_b'], 'L0_xattn_w1': _L0_xattn_in['w1'], 'L0_xattn_b1': _L0_xattn_in['b1'], 'L0_xattn_w2': _L0_xattn_in['w2'], 'L0_xattn_b2': _L0_xattn_in['b2'], 'L1_xattn_ln1_w': _L1_xattn_in['ln1_w'], 'L1_xattn_ln1_b': _L1_xattn_in['ln1_b'], 'L1_xattn_ln2_w': _L1_xattn_in['ln2_w'], 'L1_xattn_ln2_b': _L1_xattn_in['ln2_b'], 'L1_xattn_maa_x': _L1_xattn_in['maa_x'], 'L1_xattn_maa_w1': _L1_xattn_in['maa_w1'], 'L1_xattn_maa_w2': _L1_xattn_in['maa_w2'], 'L1_xattn_maa_stack': _L1_xattn_in['maa_stack'], 'L1_xattn_time_decay': _L1_xattn_in['time_decay'], 'L1_xattn_td_w1': _L1_xattn_in['td_w1'], 'L1_xattn_td_w2': _L1_xattn_in['td_w2'], 'L1_xattn_u': _L1_xattn_in['u'], 'L1_xattn_Wr': _L1_xattn_in['Wr'], 'L1_xattn_Wk': _L1_xattn_in['Wk'], 'L1_xattn_Wv': _L1_xattn_in['Wv'], 'L1_xattn_Wg': _L1_xattn_in['Wg'], 'L1_xattn_Wo': _L1_xattn_in['Wo'], 'L1_xattn_gn_w': _L1_xattn_in['gn_w'], 'L1_xattn_gn_b': _L1_xattn_in['gn_b'], 'L1_xattn_ffn_maa_k': _L1_xattn_in['ffn_maa_k'], 'L1_xattn_ffn_maa_r': _L1_xattn_in['ffn_maa_r'], 'L1_xattn_Wfk': _L1_xattn_in['Wfk'], 'L1_xattn_Wfr': _L1_xattn_in['Wfr'], 'L1_xattn_Wfv': _L1_xattn_in['Wfv']}

def reference(x, ctx_2048, mask_1x1xSxS2_fc1, mask_Bx1xSxS2_ff1, L0_xattn_ln1_s, L0_xattn_ln1_b, L0_xattn_w_qkv, L0_xattn_b_qkv, L0_xattn_w_ao, L0_xattn_b_ao, L0_xattn_ln2_s, L0_xattn_ln2_b, L0_xattn_w_q, L0_xattn_b_q, L0_xattn_w_kv, L0_xattn_b_kv, L0_xattn_w_co, L0_xattn_b_co, L0_xattn_ln3_s, L0_xattn_ln3_b, L0_xattn_w1, L0_xattn_b1, L0_xattn_w2, L0_xattn_b2, L1_xattn_ln1_w, L1_xattn_ln1_b, L1_xattn_ln2_w, L1_xattn_ln2_b, L1_xattn_maa_x, L1_xattn_maa_w1, L1_xattn_maa_w2, L1_xattn_maa_stack, L1_xattn_time_decay, L1_xattn_td_w1, L1_xattn_td_w2, L1_xattn_u, L1_xattn_Wr, L1_xattn_Wk, L1_xattn_Wv, L1_xattn_Wg, L1_xattn_Wo, L1_xattn_gn_w, L1_xattn_gn_b, L1_xattn_ffn_maa_k, L1_xattn_ffn_maa_r, L1_xattn_Wfk, L1_xattn_Wfr, L1_xattn_Wfv):
    import jax
    import jax.numpy as jnp

    def _L0_xattn_ref(hidden_states, encoder_states, ltor_mask, cross_mask, ln1_s, ln1_b, w_qkv, b_qkv, w_ao, b_ao, ln2_s, ln2_b, w_q, b_q, w_kv, b_kv, w_co, b_co, ln3_s, ln3_b, w1, b1, w2, b2):
        import jax, jax.numpy as jnp
        import numpy as np
        H = 512
        NH = 16
        HD = H // NH
        EPS = 1e-05

        def gelu(x):
            return 0.5 * x * (1.0 + jnp.tanh(0.7978845608028654 * x * (1.0 + 0.044715 * x * x)))

        def layernorm(x, scale, bias):
            m = jnp.mean(x, axis=-1, keepdims=True)
            v = jnp.mean(jnp.square(x - m), axis=-1, keepdims=True)
            return (x - m) * jax.lax.rsqrt(v + EPS) * scale + bias

        def split_heads(x):
            b, s, _ = x.shape
            return x.reshape(b, s, NH, HD).transpose(0, 2, 1, 3)

        def merge_heads(x):
            b, nh, s, hd = x.shape
            return x.transpose(0, 2, 1, 3).reshape(b, s, nh * hd)

        def attention(q, k, v, mask):
            scores = jnp.einsum('bhqd,bhkd->bhqk', q, k) / jnp.sqrt(jnp.float32(HD))
            scores = scores * mask - 10000.0 * (1.0 - mask)
            probs = jax.nn.softmax(scores, axis=-1)
            return jnp.einsum('bhqk,bhkd->bhqd', probs, v)
        ln_out = layernorm(hidden_states, ln1_s, ln1_b)
        qkv = ln_out @ w_qkv + b_qkv
        q, k, v = jnp.split(qkv, 3, axis=-1)
        ctx = merge_heads(attention(split_heads(q), split_heads(k), split_heads(v), ltor_mask))
        attn_out = ctx @ w_ao + b_ao
        x = hidden_states + attn_out
        ln_out = layernorm(x, ln2_s, ln2_b)
        q = ln_out @ w_q + b_q
        kv = encoder_states @ w_kv + b_kv
        k, v = jnp.split(kv, 2, axis=-1)
        ctx = merge_heads(attention(split_heads(q), split_heads(k), split_heads(v), cross_mask))
        cross_out = ctx @ w_co + b_co
        x = x + cross_out
        ln_out = layernorm(x, ln3_s, ln3_b)
        mlp_out = gelu(ln_out @ w1 + b1) @ w2 + b2
        return x + mlp_out

    def _L1_xattn_ref(x, state, ln1_w, ln1_b, ln2_w, ln2_b, maa_x, maa_w1, maa_w2, maa_stack, time_decay, td_w1, td_w2, u, Wr, Wk, Wv, Wg, Wo, gn_w, gn_b, ffn_maa_k, ffn_maa_r, Wfk, Wfr, Wfv):
        import jax, jax.numpy as jnp
        import numpy as np
        E, H, L, B = (512, 32, 256, 4)
        S = E // H
        DM, DD = (32, 64)

        def _ln(x, w, b, eps=1e-05):
            m = x.mean(-1, keepdims=True)
            v = ((x - m) ** 2).mean(-1, keepdims=True)
            return (x - m) / jnp.sqrt(v + eps) * w + b

        def _block(x, state, ln1_w, ln1_b, ln2_w, ln2_b, maa_x, maa_w1, maa_w2, maa_stack, time_decay, td_w1, td_w2, u, Wr, Wk, Wv, Wg, Wo, gn_w, gn_b, ffn_maa_k, ffn_maa_r, Wfk, Wfr, Wfv):
            b, l, e = x.shape
            h = u.shape[0]
            s_ = e // h
            xa = _ln(x, ln1_w, ln1_b)
            sx = jnp.concatenate([state[:, 1:2] - xa[:, :1], xa[:, :-1] - xa[:, 1:]], axis=1)
            xxx = jnp.tanh((xa + sx * maa_x) @ maa_w1).reshape(b, l, 5, DM)
            xxx = jnp.einsum('blfd,fde->blfe', xxx, maa_w2)
            xm = xa[:, :, None] + sx[:, :, None] * (maa_stack + xxx)
            xk, xw, xv, xr, xg = (xm[:, :, j] for j in range(5))
            w = jnp.exp(-jnp.exp(time_decay + jnp.tanh(xw @ td_w1) @ td_w2)).reshape(b, l, h, s_)
            r = (xr @ Wr.T).reshape(b, l, h, s_)
            k = (xk @ Wk.T).reshape(b, l, h, s_)
            v = (xv @ Wv.T).reshape(b, l, h, s_)
            g = jax.nn.silu(xg @ Wg.T)
            s0 = state[:, 2:2 + s_].reshape(b, h, s_, s_)

            def step(s, rkvw):
                r_t, k_t, v_t, w_t = rkvw
                a = k_t[..., :, None] * v_t[..., None, :]
                out = jnp.einsum('bhi,bhij->bhj', r_t, u * a + s)
                s = a + w_t[..., :, None] * s
                return (s, out)
            rkvw = tuple((jnp.moveaxis(t, 1, 0) for t in (r, k, v, w)))
            _, out = jax.lax.scan(step, s0, rkvw)
            out = jnp.moveaxis(out, 0, 1).reshape(b, l, e)
            og = out.reshape(b, l, h, s_)
            m = og.mean(-1, keepdims=True)
            va = ((og - m) ** 2).mean(-1, keepdims=True)
            og = ((og - m) / jnp.sqrt(va + 1e-05)).reshape(b, l, e) * gn_w + gn_b
            x1 = x + og * g @ Wo.T
            xc = _ln(x1, ln2_w, ln2_b)
            sx2 = jnp.concatenate([state[:, 0:1] - xc[:, :1], xc[:, :-1] - xc[:, 1:]], axis=1)
            xk2 = xc + sx2 * ffn_maa_k
            xr2 = xc + sx2 * ffn_maa_r
            rr = jax.nn.sigmoid(xr2 @ Wfr.T)
            kk = jnp.square(jax.nn.relu(xk2 @ Wfk.T))
            return x1 + rr * (kk @ Wfv.T)
        return _block(x, state, ln1_w, ln1_b, ln2_w, ln2_b, maa_x, maa_w1, maa_w2, maa_stack, time_decay, td_w1, td_w2, u, Wr, Wk, Wv, Wg, Wo, gn_w, gn_b, ffn_maa_k, ffn_maa_r, Wfk, Wfr, Wfv)
    x = _L0_xattn_ref(x, ctx_2048, mask_1x1xSxS2_fc1, mask_Bx1xSxS2_ff1, L0_xattn_ln1_s, L0_xattn_ln1_b, L0_xattn_w_qkv, L0_xattn_b_qkv, L0_xattn_w_ao, L0_xattn_b_ao, L0_xattn_ln2_s, L0_xattn_ln2_b, L0_xattn_w_q, L0_xattn_b_q, L0_xattn_w_kv, L0_xattn_b_kv, L0_xattn_w_co, L0_xattn_b_co, L0_xattn_ln3_s, L0_xattn_ln3_b, L0_xattn_w1, L0_xattn_b1, L0_xattn_w2, L0_xattn_b2)
    x = _L1_xattn_ref(x, ctx_2048, L1_xattn_ln1_w, L1_xattn_ln1_b, L1_xattn_ln2_w, L1_xattn_ln2_b, L1_xattn_maa_x, L1_xattn_maa_w1, L1_xattn_maa_w2, L1_xattn_maa_stack, L1_xattn_time_decay, L1_xattn_td_w1, L1_xattn_td_w2, L1_xattn_u, L1_xattn_Wr, L1_xattn_Wk, L1_xattn_Wv, L1_xattn_Wg, L1_xattn_Wo, L1_xattn_gn_w, L1_xattn_gn_b, L1_xattn_ffn_maa_k, L1_xattn_ffn_maa_r, L1_xattn_Wfk, L1_xattn_Wfr, L1_xattn_Wfv)
    return x

_drawn_inputs = setup_inputs


def setup_inputs(seed=0):
    import zlib

    import numpy as np

    out = dict(_drawn_inputs(seed))
    spreads = {'L0_xattn_ln1_s': (1.0, 0.6),
     'L0_xattn_ln1_b': (0.0, 0.395),
     'L0_xattn_b_qkv': (0.0, 0.1),
     'L0_xattn_b_ao': (0.0, 0.1),
     'L0_xattn_ln2_s': (1.0, 0.6),
     'L0_xattn_ln2_b': (0.0, 2.0),
     'L0_xattn_b_q': (0.0, 2.0),
     'L0_xattn_b_kv': (0.0, 0.1),
     'L0_xattn_b_co': (0.0, 0.1),
     'L0_xattn_ln3_s': (1.0, 0.2),
     'L0_xattn_ln3_b': (0.0, 0.319),
     'L0_xattn_b1': (0.0, 0.1),
     'L0_xattn_b2': (0.0, 0.1),
     'L1_xattn_ln1_w': (1.0, 0.2),
     'L1_xattn_ln1_b': (0.0, 0.288),
     'L1_xattn_ln2_w': (1.0, 0.6),
     'L1_xattn_ln2_b': (0.0, 0.8),
     'L1_xattn_gn_w': (1.0, 0.6),
     'L1_xattn_gn_b': (0.0, 0.754)}
    factors = {'L0_xattn_w_q': 64.0,
     'L1_xattn_maa_x': 8.0,
     'L1_xattn_maa_w1': 3.172,
     'L1_xattn_maa_w2': 3.155,
     'L1_xattn_td_w1': 8.0,
     'L1_xattn_td_w2': 8.0,
     'L1_xattn_u': 3.189,
     'L1_xattn_ffn_maa_k': 6.172,
     'L1_xattn_ffn_maa_r': 8.0,
     'L1_xattn_Wfr': 4.36}
    for name, (base, spread) in spreads.items():
        noise = np.random.default_rng([zlib.crc32(name.encode()), seed]).standard_normal(out[name].shape)
        drawn = base * np.exp(spread * noise) if base else spread * noise
        out[name] = jnp.asarray(drawn.astype(out[name].dtype))
    for name, factor in factors.items():
        out[name] = (out[name] * factor).astype(out[name].dtype)
    return out
```

```python
from contextlib import ExitStack

import concourse.bass as bass
from concourse import mybir

F32 = mybir.dt.float32
ALU = mybir.AluOpType
ACT = mybir.ActivationFunctionType
AX_X = mybir.AxisListType.X

P = 128
BATCH, SEQ, DM = 8, 256, 512
TT = SEQ // P
CG = DM // P
NH, HD = 16, 32
HPG = P // HD
FF = 4 * DM
FQ = 4
EPS = 1e-5
MASKED = 10000.0
SCORE_SCALE = float(HD) ** -0.5


class Tally:

    def __init__(self, sem, per, unit=1, by=None):
        self.sem, self.per, self.unit, self.by = sem, per, unit, by
        self.start = unit if by else 0

    def at(self, b, k):
        assert k or self.by
        return b * (self.per * self.unit) + (k * self.unit + self.start)

    def prime(self, eng):
        eng.sem_inc(self.sem, self.unit)


def attention_block(nc, sems, T, x3_dram):
    with ExitStack() as ctx:
        def sb(name, *shape):
            return ctx.enter_context(nc.sbuf_tensor("a_" + name, list(shape), F32))

        def sem(name):
            return sems.enter_context(nc.semaphore("a_" + name))

        def psum(name):
            return ctx.enter_context(nc.psum_tensor("a_" + name, [P, 512], F32))

        w_qkv = sb("w_qkv", P, CG, 3 * DM)
        w_ao = sb("w_ao", P, CG, DM)
        w_q = sb("w_q", P, CG, DM)
        w_kv = sb("w_kv", P, CG, 2 * DM)
        w_co = sb("w_co", P, CG, DM)
        ring = sb("ring", P, 2, CG * DM)
        vec = sb("vec", P, len(T["vecs_a"]), CG)
        b1_col = sb("b1_col", P, FF // P)
        head_row = sb("head_row", P, HPG)
        ident = sb("ident", P, P)
        bias_all = sb("bias_all", P, 3, DM)
        mask = sb("mask", P, 2, TT * SEQ)
        fill = sb("fill", P, 2, TT * SEQ)
        x_new = sb("x_new", P, TT * DM)
        x = sb("x", P, TT * DM)
        enc = sb("enc", P, TT * DM)
        xb = sb("xb", P, TT * DM)
        h = sb("h", P, TT * DM)
        hT = sb("hT", P, CG, SEQ)
        encT = sb("encT", P, CG, SEQ)
        qT = sb("qT", P, CG, SEQ)
        kT = sb("kT", P, CG, SEQ)
        k_head = sb("k_head", P, 2, HPG, SEQ)
        v = sb("v", P, 2, TT * DM)
        ctxT = sb("ctxT", P, CG, SEQ)
        score = sb("score", P, 2, TT * SEQ)
        prob = sb("prob", P, 4, TT * SEQ)
        probT = sb("probT", P, 2, 2 * SEQ)
        f1T = sb("f1T", P, 2, CG, SEQ)
        low = sb("low", P, NH, TT)
        rowsum = sb("rowsum", P, NH, TT)
        rowinv = sb("rowinv", P, NH, TT)
        stats = sb("stats", P, TT, 6)
        meanvar = sb("meanvar", P, TT, 2)
        std = sb("std", P, TT)
        rstd = sb("rstd", P, TT)
        eps_col = sb("eps_col", P, 1)

        G = [psum("G0"), psum("G1")]
        S = [psum("S0"), psum("S1")]
        PT = [psum("PT0"), psum("PT1")]
        O = [psum("O0"), psum("O1")]

        G_TILES = (["encT"] * 2 + ["hT1"] * 2 + ["q"] * 2 + ["k"] * 2 + ["v"] * 2 + ["xk"] * 2 + ["xv"] * 2
                   + ["ao"] * 2 + ["hT2"] * 2 + ["xq"] * 2 + ["co"] * 2 + ["hT3"] * 2 + ["f1"] * (2 * FQ))
        TAKER = {"encT": "act", "hT1": "act", "hT2": "act", "hT3": "act", "k": "act", "xk": "act", "f1": "act",
                 "q": "dve", "xq": "dve", "v": "dve", "xv": "dve", "ao": "dve", "co": "dve"}
        NG = len(G_TILES)
        takers = [TAKER[t] for t in G_TILES]

        weights_in = sem("weights_in")
        consts_made = sem("consts_made")
        self_filled = sem("self_filled")
        x_in = Tally(sem("x_in"), 1, 16)
        enc_in = Tally(sem("enc_in"), 1, 16)
        mask_in = Tally(sem("mask_in"), 1, 16)
        ring_in = [Tally(sem(f"ring_in{i}"), FQ, 16) for i in range(2)]
        w2_used = Tally(sem("w2_used"), FQ - 1)
        g_full = Tally(sem("g_full"), NG, by="pe")
        g_taken = {e: Tally(sem("g_taken_" + e), takers.count(e), by=e) for e in ("act", "dve")}
        s_full = Tally(sem("s_full"), 2 * NH)
        s_taken = Tally(sem("s_taken"), 2 * NH, by="dve")
        pt_full = Tally(sem("pt_full"), 2 * NH)
        pt_taken = Tally(sem("pt_taken"), 2 * NH, by="act")
        o_full = Tally(sem("o_full"), 2 * CG + TT, by="pe")
        o_taken = Tally(sem("o_taken"), 2 * CG + TT, by="dve")
        filled = Tally(sem("filled"), 1)
        low_made = Tally(sem("low_made"), 2 * NH, by="dve")
        exp_done = Tally(sem("exp_done"), 2 * NH)
        inv_made = Tally(sem("inv_made"), 2 * NH)
        prob_made = Tally(sem("prob_made"), 2 * NH)
        khead_made = Tally(sem("khead_made"), 2 * NH)
        var_made = Tally(sem("var_made"), 3)
        std_made = Tally(sem("std_made"), 3)
        h_made = Tally(sem("h_made"), 3 * TT, by="dve")
        xb_made = Tally(sem("xb_made"), 3, by="pool")
        x_out = Tally(sem("x_out"), 1, 16, by="act")
        links = Tally(sem("dve_links"), 3 * (TT + 1) + 1)

        def alone(eng):
            eng.nop(nofuse=True)

        first_g = {}
        for n, name in enumerate(G_TILES):
            first_g.setdefault(name, n)

        def g_taken_by(b, n):
            who = takers[n]
            return g_taken[who].sem, g_taken[who].at(b, takers[:n + 1].count(who))

        def g_free(b, n):
            if n >= 2:
                return g_taken_by(b, n - 2)
            return g_taken[takers[-1]].sem, g_taken[takers[-1]].at(b, 0)

        def taken(b, name, k):
            return g_taken_by(b, first_g[name] + k)

        vi = {name: i for i, name in enumerate(T["vecs_a"])}
        block = ctx.enter_context(nc.Block())

        N_WEIGHT_DMAS = 5 + len(T["vecs_a"]) + 1 + 1 + 3

        @block.sync
        def _(sp):
            for name, tile in (("w_qkv", w_qkv), ("w_ao", w_ao), ("w_q", w_q), ("w_kv", w_kv), ("w_co", w_co)):
                sp.dma_start(tile[:, :, :], T[name].rearrange("(c p) n -> p c n", p=P)).then_inc(weights_in, 16)
            sp.dma_start(mask[:, 0, :].rearrange("p (a k) -> p a k", a=TT),
                         T["mask_self"].rearrange("(a p) k -> p a k", p=P)).then_inc(weights_in, 16)
            with nc.allow_non_contiguous_dma(reason="channel vectors, once"):
                for name, i in vi.items():
                    sp.dma_start(vec[:, i, :], T[name].rearrange("(c p) -> p c", p=P)).then_inc(weights_in, 16)
                sp.dma_start(b1_col[:, :], T["b1"].rearrange("(c p) -> p c", p=P)).then_inc(weights_in, 16)
            for i, name in enumerate(("b_ao", "b_co", "b2")):
                sp.dma_start(bias_all[:, i, :], T[name].rearrange("(a n) -> a n", a=1).to_broadcast([P, DM]))\
                    .then_inc(weights_in, 16)
            with sp.Fori(0, BATCH) as b:
                sp.wait_ge(xb_made.sem, xb_made.at(b, 0))
                alone(sp)
                sp.wait_ge(h_made.sem, h_made.at(b, 0))
                alone(sp)
                sp.dma_start(x_new[:, :].rearrange("p (a n) -> p a n", a=TT),
                             T["x"][b, :, :].rearrange("(a p) n -> p a n", p=P)).then_inc(x_in.sem, 16)
                sp.wait_ge(g_full.sem, g_full.at(b, 0))
                alone(sp)
                sp.dma_start(enc[:, :].rearrange("p (a n) -> p a n", a=TT),
                             T["enc"][b, :, :].rearrange("(a p) n -> p a n", p=P)).then_inc(enc_in.sem, 16)
                sp.wait_ge(low_made.sem, low_made.at(b, 0))
                alone(sp)
                sp.dma_start(mask[:, 1, :].rearrange("p (a k) -> p a k", a=TT),
                             T["mask_cross"][b, :, :].rearrange("(a p) k -> p a k", p=P)).then_inc(mask_in.sem, 16)
                for quarter in range(FQ):
                    if quarter:
                        sp.wait_ge(g_full.sem, g_full.at(b, first_g["f1"] + 2 * quarter))
                    alone(sp)
                    sp.dma_start(ring[:, 0, :].rearrange("p (c n) -> p c n", c=CG),
                                 T["w1"].rearrange("(c p) n -> p c n", p=P)[:, :, quarter * DM:(quarter + 1) * DM])\
                        .then_inc(ring_in[0].sem, 16)
                    if quarter:
                        sp.wait_ge(w2_used.sem, w2_used.at(b, quarter))
                        alone(sp)
                    else:
                        sp.wait_ge(o_full.sem, o_full.at(b, 0))
                    alone(sp)
                    sp.dma_start(ring[:, 1, :].rearrange("p (c n) -> p c n", c=CG),
                                 T["w2"][quarter * DM:(quarter + 1) * DM, :].rearrange("(c p) n -> p c n", p=P))\
                        .then_inc(ring_in[1].sem, 16)

        @block.gpsimd
        def _(pool):
            nc.gpsimd.memset(ident[:, :], 0.0).then_inc(consts_made, 1)
            nc.gpsimd.memset(eps_col[:, :], EPS)
            nc.gpsimd.memset(head_row[:, :], 1.0).then_inc(consts_made, 1)
            pool.wait_ge(consts_made, 2)
            nc.gpsimd.affine_select(out=ident[:, :], in_=ident[:, :], compare_op=ALU.not_equal, fill=1.0, base=0,
                                    pattern=[[-1, P]], channel_multiplier=1).then_inc(consts_made, 1)
            nc.gpsimd.affine_select(out=head_row[:, :], in_=head_row[:, :], compare_op=ALU.is_ge, fill=0.0, base=0,
                                    pattern=[[-HD, HPG]], channel_multiplier=1).then_inc(consts_made, 1)
            pool.wait_ge(consts_made, 4)
            nc.gpsimd.affine_select(out=head_row[:, :], in_=head_row[:, :], compare_op=ALU.is_ge, fill=0.0,
                                    base=HD - 1, pattern=[[HD, HPG]], channel_multiplier=-1).then_inc(consts_made, 1)
            pool.wait_ge(consts_made, 5)
            pool.wait_ge(weights_in, 16 * N_WEIGHT_DMAS)

            def add_bias(b, i, src):
                nc.gpsimd.tensor_tensor(xb[:, :].rearrange("p (a n) -> p a n", a=TT),
                                        src.rearrange("p (a n) -> p a n", a=TT),
                                        bias_all[:, i:i + 1, :].to_broadcast([P, TT, DM]), ALU.add)\
                    .then_inc(xb_made.sem, 1)

            def heads(b, at):
                def khead(hh):
                    g, j = hh // HPG, hh % HPG
                    if j == 0:
                        if at or g >= 2:
                            pool.wait_ge(s_full.sem, s_full.at(b, at * NH + (g - 1) * HPG))
                    if hh == 0:
                        pool.wait_ge(*taken(b, "xk" if at else "k", 0))
                    if hh == 2 * HPG:
                        pool.wait_ge(*taken(b, "xk" if at else "k", 1))
                    alone(pool)
                    nc.gpsimd.tensor_scalar(k_head[:, g % 2, j, :], kT[:, g, :], head_row[:, j:j + 1], None, ALU.mult)\
                        .then_inc(khead_made.sem, 1)

                for i in range(NH + 4):
                    if i < NH:
                        khead(i)
                    if i >= 4:
                        hh = i - 4
                        pool.wait_ge(inv_made.sem, inv_made.at(b, at * NH + hh + 1))
                        alone(pool)
                        for a in range(TT):
                            q = prob[:, hh % 4, a * SEQ:(a + 1) * SEQ]
                            last = nc.gpsimd.tensor_scalar(q, q, rowinv[:, hh, a:a + 1], None, ALU.mult)
                        last.then_inc(prob_made.sem, 1)

            for tally in (xb_made,):
                tally.prime(pool)
            with pool.Fori(0, BATCH) as b:
                pool.wait_ge(x_in.sem, x_in.at(b, 1))
                pool.wait_ge(o_taken.sem, o_taken.at(b, 0))
                add_bias(b, 0, x_new[:, :])
                heads(b, 0)
                pool.wait_ge(*taken(b, "ao", 1))
                add_bias(b, 1, x[:, :])
                heads(b, 1)
                pool.wait_ge(*taken(b, "co", 1))
                add_bias(b, 2, x[:, :])

        @block.tensor
        def _(pe):
            pe.wait_ge(weights_in, 16 * N_WEIGHT_DMAS)
            pe.wait_ge(consts_made, 5)

            def turn(b, n, src):
                pair = n % 2
                pe.wait_ge(*g_free(b, n))
                for c in range(2):
                    for a in range(TT):
                        col = (2 * pair + c) * P
                        last = nc.tensor.transpose(G[n % 2][:, c * SEQ + a * P:c * SEQ + (a + 1) * P],
                                                   src[:, a * DM + col:a * DM + col + P], ident[:, :])
                last.then_inc(g_full.sem, 1)

            def project_T(b, n, w, col, actT):
                pe.wait_ge(*g_free(b, n))
                for m in range(2):
                    for c in range(CG):
                        last = nc.tensor.matmul(G[n % 2][:, m * SEQ:(m + 1) * SEQ],
                                                w[:, c, col + m * P:col + (m + 1) * P], actT[:, c, :],
                                                start=(c == 0), stop=(c == CG - 1))
                last.then_inc(g_full.sem, 1)

            def project(b, n, w, col, actT, a):
                pe.wait_ge(*g_free(b, n))
                for c in range(CG):
                    last = nc.tensor.matmul(G[n % 2][:, :], actT[:, c, a * P:(a + 1) * P], w[:, c, col:col + DM],
                                            start=(c == 0), stop=(c == CG - 1))
                last.then_inc(g_full.sem, 1)

            def attend(b, at):
                def scores(hh):
                    n = at * NH + hh
                    g, j = hh // HPG, hh % HPG
                    if hh == 0 or hh == 2 * HPG:
                        pe.wait_ge(*taken(b, "xq" if at else "q", g // 2))
                    pe.wait_ge(khead_made.sem, khead_made.at(b, n + 1))
                    pe.wait_ge(s_taken.sem, s_taken.at(b, max(n - 1, 0)))
                    for a in range(TT):
                        last = nc.tensor.matmul(S[n % 2][:, a * SEQ:(a + 1) * SEQ], qT[:, g, a * P:(a + 1) * P],
                                                k_head[:, g % 2, j, :], start=True, stop=True)
                    last.then_inc(s_full.sem, 1)

                def turn_probs(hh):
                    n = at * NH + hh
                    pe.wait_ge(prob_made.sem, prob_made.at(b, n + 1))
                    pe.wait_ge(pt_taken.sem, pt_taken.at(b, max(n - 1, 0)))
                    for k in range(2):
                        for a in range(TT):
                            last = nc.tensor.transpose(PT[n % 2][:, k * SEQ + a * P:k * SEQ + (a + 1) * P],
                                                       prob[:, hh % 4, a * SEQ + k * P:a * SEQ + (k + 1) * P],
                                                       ident[:, :])
                    last.then_inc(pt_full.sem, 1)

                def contexts(hh):
                    n = at * NH + hh
                    g, j = hh // HPG, hh % HPG
                    pe.wait_ge(pt_taken.sem, pt_taken.at(b, n + 1))
                    if j == 0:
                        pe.wait_ge(o_taken.sem, o_taken.at(b, max(at * CG + g - 1, 0)))
                    if hh == 0:
                        pe.wait_ge(*taken(b, "xv" if at else "v", 1))
                    for k in range(2):
                        last = nc.tensor.matmul(O[g % 2][j * HD:(j + 1) * HD, 0:SEQ],
                                                v[:, at, k * DM + hh * HD:k * DM + (hh + 1) * HD],
                                                probT[:, n % 2, k * SEQ:(k + 1) * SEQ],
                                                start=(k == 0), stop=(k == 1))
                    if j == HPG - 1:
                        last.then_inc(o_full.sem, 1)

                for i in range(NH + 5):
                    if i < NH:
                        scores(i)
                    if 4 <= i < NH + 4:
                        turn_probs(i - 4)
                    if i >= 5:
                        contexts(i - 5)

            for tally in (g_full, o_full,):
                tally.prime(pe)
            with pe.Fori(0, BATCH) as b:
                pe.wait_ge(enc_in.sem, enc_in.at(b, 1))
                for k in range(2):
                    turn(b, first_g["encT"] + k, enc)
                pe.wait_ge(h_made.sem, h_made.at(b, TT))
                for k in range(2):
                    turn(b, first_g["hT1"] + k, h)
                pe.wait_ge(*taken(b, "hT1", 1))
                for k in range(2):
                    project_T(b, first_g["q"] + k, w_qkv, k * 2 * P, hT)
                for k in range(2):
                    project_T(b, first_g["k"] + k, w_qkv, DM + k * 2 * P, hT)
                for k in range(TT):
                    project(b, first_g["v"] + k, w_qkv, 2 * DM, hT, k)
                attend(b, 0)
                for k in range(2):
                    project_T(b, first_g["xk"] + k, w_kv, k * 2 * P, encT)
                for k in range(TT):
                    project(b, first_g["xv"] + k, w_kv, DM, encT, k)
                pe.wait_ge(o_taken.sem, o_taken.at(b, CG))
                for k in range(TT):
                    project(b, first_g["ao"] + k, w_ao, 0, ctxT, k)
                pe.wait_ge(h_made.sem, h_made.at(b, 2 * TT))
                for k in range(2):
                    turn(b, first_g["hT2"] + k, h)
                pe.wait_ge(*taken(b, "hT2", 1))
                for k in range(2):
                    project_T(b, first_g["xq"] + k, w_q, k * 2 * P, hT)
                attend(b, 1)
                pe.wait_ge(o_taken.sem, o_taken.at(b, 2 * CG))
                for k in range(TT):
                    project(b, first_g["co"] + k, w_co, 0, ctxT, k)
                pe.wait_ge(h_made.sem, h_made.at(b, 3 * TT))
                for k in range(2):
                    turn(b, first_g["hT3"] + k, h)
                pe.wait_ge(*taken(b, "hT3", 1))

                def hidden(quarter):
                    pe.wait_ge(ring_in[0].sem, ring_in[0].at(b, quarter + 1))
                    for k in range(2):
                        n = first_g["f1"] + 2 * quarter + k
                        project_T(b, n, ring[:, 0, :].rearrange("p (c n) -> p c n", c=CG), k * 2 * P, hT)

                def output(quarter):
                    pe.wait_ge(ring_in[1].sem, ring_in[1].at(b, quarter + 1))
                    pe.wait_ge(*taken(b, "f1", 2 * quarter + 1))
                    w2 = ring[:, 1, :].rearrange("p (c n) -> p c n", c=CG)
                    for a in range(TT):
                        for c in range(CG):
                            last = nc.tensor.matmul(O[a][:, :], f1T[:, quarter % 2, c, a * P:(a + 1) * P], w2[:, c, :],
                                                    start=(quarter == 0 and c == 0),
                                                    stop=(quarter == FQ - 1 and c == CG - 1))
                        if quarter == FQ - 1:
                            last.then_inc(o_full.sem, 1)
                    if quarter < FQ - 1:
                        last.then_inc(w2_used.sem, 1)

                hidden(0)
                for quarter in range(FQ):
                    output(quarter)
                    if quarter + 1 < FQ:
                        hidden(quarter + 1)

        @block.vector
        def _(dve):
            dve.wait_ge(weights_in, 16 * N_WEIGHT_DMAS)
            nc.vector.tensor_scalar(fill[:, 0, :], mask[:, 0, :], -MASKED, MASKED, ALU.mult, ALU.add)\
                .then_inc(self_filled, 1)
            dve.wait_ge(self_filled, 1)
            count = [0]

            def link(b, ins):
                count[0] += 1
                ins.then_inc(links.sem, 1)
                dve.wait_ge(links.sem, links.at(b, count[0]))

            def layernorm(b, i, src):
                for a in range(TT):
                    link(b, nc.vector.bn_stats(stats[:, a, :], src[:, a * DM:(a + 1) * DM]))
                alone(dve)
                for a in range(TT):
                    last = nc.vector.bn_aggr(meanvar[:, a, :], stats[:, a, :])
                last.then_inc(var_made.sem, 1)
                dve.wait_ge(std_made.sem, std_made.at(b, i + 1))
                link(b, nc.vector.reciprocal(rstd[:, :], std[:, :]))
                for a in range(TT):
                    nc.vector.tensor_scalar(h[:, a * DM:(a + 1) * DM], src[:, a * DM:(a + 1) * DM],
                                            meanvar[:, a, 0:1], rstd[:, a:a + 1], ALU.subtract, ALU.mult)\
                        .then_inc(h_made.sem, 1)

            def take_q(b, name, bias):
                for k in range(2):
                    n = first_g[name] + k
                    dve.wait_ge(g_full.sem, g_full.at(b, n + 1))
                    for m in range(2):
                        last = nc.vector.tensor_scalar(qT[:, 2 * k + m, :], G[n % 2][:, m * SEQ:(m + 1) * SEQ],
                                                       vec[:, vi[bias], 2 * k + m:2 * k + m + 1], None, ALU.add)
                    last.then_inc(g_taken["dve"].sem, 1)

            def take_v(b, name, at):
                for k in range(TT):
                    n = first_g[name] + k
                    dve.wait_ge(g_full.sem, g_full.at(b, n + 1))
                    nc.vector.tensor_copy(v[:, at, k * DM:(k + 1) * DM], G[n % 2][:, :])\
                        .then_inc(g_taken["dve"].sem, 1)

            def take_x(b, name):
                for k in range(TT):
                    n = first_g[name] + k
                    dve.wait_ge(g_full.sem, g_full.at(b, n + 1))
                    nc.vector.tensor_tensor(x[:, k * DM:(k + 1) * DM], G[n % 2][:, :], xb[:, k * DM:(k + 1) * DM],
                                            ALU.add).then_inc(g_taken["dve"].sem, 1)

            def attend(b, at, bias):
                def invert(hh):
                    n = at * NH + hh
                    dve.wait_ge(exp_done.sem, exp_done.at(b, n + 1))
                    return nc.vector.reciprocal(rowinv[:, hh, :], rowsum[:, hh, :])

                def take_context(g):
                    dve.wait_ge(o_full.sem, o_full.at(b, at * CG + g + 1))
                    nc.vector.tensor_scalar(ctxT[:, g, :], O[g % 2][:, 0:SEQ], vec[:, vi[bias], g:g + 1], None,
                                            ALU.add).then_inc(o_taken.sem, 1)

                for i in range(NH):
                    n = at * NH + i
                    dve.wait_ge(s_full.sem, s_full.at(b, n + 1))
                    if n >= 2:
                        dve.wait_ge(exp_done.sem, exp_done.at(b, n - 1))
                    nc.vector.scalar_tensor_tensor(out=score[:, i % 2, :], in0=S[n % 2][:, :], scalar=-SCORE_SCALE,
                                                   in1=mask[:, at, :], op0=ALU.mult, op1=ALU.mult)\
                        .then_inc(s_taken.sem, 1)
                    if i < 2:
                        dve.wait_ge(s_taken.sem, s_taken.at(b, n + 1))
                        alone(dve)
                    else:
                        dve.wait_ge(s_taken.sem, s_taken.at(b, n + 1))
                        invert(i - 2).then_inc(inv_made.sem, 1)
                    for a in range(TT):
                        sc = score[:, i % 2, a * SEQ:(a + 1) * SEQ]
                        last = nc.vector.tensor_tensor_reduce(sc, sc, fill[:, at, a * SEQ:(a + 1) * SEQ], 1.0, 3.0e38,
                                                              ALU.add, ALU.min, low[:, i, a:a + 1])
                    last.then_inc(low_made.sem, 1)
                    if i >= 9 and (i - 9) % HPG == 0:
                        take_context((i - 9) // HPG)
                for i in (NH - 2, NH - 1):
                    invert(i).then_inc(inv_made.sem, 1)
                for g in range(2, CG):
                    take_context(g)

            for tally in (g_taken["dve"], h_made, low_made, o_taken, s_taken,):
                tally.prime(dve)
            with dve.Fori(0, BATCH) as b:
                count[0] = 0
                dve.wait_ge(x_in.sem, x_in.at(b, 1))
                layernorm(b, 0, x_new)
                take_q(b, "q", "b_q1")
                take_v(b, "v", 0)
                attend(b, 0, "b_v1")
                take_v(b, "xv", 1)
                dve.wait_ge(xb_made.sem, xb_made.at(b, 1))
                dve.wait_ge(x_out.sem, x_out.at(b, 0))
                take_x(b, "ao")
                dve.wait_ge(g_taken["dve"].sem, g_taken["dve"].at(b, takers[:first_g["ao"] + 2].count("dve")))
                layernorm(b, 1, x)
                take_q(b, "xq", "b_q")
                dve.wait_ge(mask_in.sem, mask_in.at(b, 1))
                link(b, nc.vector.tensor_scalar(fill[:, 1, :], mask[:, 1, :], -MASKED, MASKED, ALU.mult, ALU.add))
                attend(b, 1, "b_v2")
                dve.wait_ge(xb_made.sem, xb_made.at(b, 2))
                take_x(b, "co")
                dve.wait_ge(g_taken["dve"].sem, g_taken["dve"].at(b, takers[:first_g["co"] + 2].count("dve")))
                layernorm(b, 2, x)
                dve.wait_ge(xb_made.sem, xb_made.at(b, 3))
                for a in range(TT):
                    dve.wait_ge(o_full.sem, o_full.at(b, 2 * CG + a + 1))
                    nc.vector.tensor_tensor(x[:, a * DM:(a + 1) * DM], O[a][:, :], xb[:, a * DM:(a + 1) * DM],
                                            ALU.add).then_inc(o_taken.sem, 1)
                assert count[0] == links.per, count

        @block.scalar
        def _(act):
            act.wait_ge(weights_in, 16 * N_WEIGHT_DMAS)
            act.wait_ge(consts_made, 5)

            def root(b, i):
                act.wait_ge(var_made.sem, var_made.at(b, i + 1))
                nc.scalar.activation(std[:, :], meanvar[:, :, 1], ACT.Sqrt, bias=eps_col[:, :]).then_inc(std_made.sem, 1)

            def take_T(b, name, dst, scale, bias):
                for k in range(2):
                    n = first_g[name] + k
                    act.wait_ge(g_full.sem, g_full.at(b, n + 1))
                    if scale is None and bias is None:
                        last = nc.scalar.activation(dst[:, 2 * k:2 * k + 2, :].rearrange("p c t -> p (c t)"),
                                                    G[n % 2][:, :], ACT.Copy)
                    else:
                        for m in range(2):
                            c = 2 * k + m
                            last = nc.scalar.activation(dst[:, c, :], G[n % 2][:, m * SEQ:(m + 1) * SEQ], ACT.Identity,
                                                        bias=vec[:, vi[bias], c:c + 1],
                                                        scale=1.0 if scale is None else vec[:, vi[scale], c:c + 1])
                    last.then_inc(g_taken["act"].sem, 1)

            def attend(b, at):
                def exponentials(hh):
                    n = at * NH + hh
                    act.wait_ge(low_made.sem, low_made.at(b, n + 1))
                    if n >= 4:
                        act.wait_ge(pt_full.sem, pt_full.at(b, n - 3))
                    for a in range(TT):
                        last = nc.scalar.activation(prob[:, hh % 4, a * SEQ:(a + 1) * SEQ],
                                                    score[:, hh % 2, a * SEQ:(a + 1) * SEQ], ACT.Exp,
                                                    bias=low[:, hh, a:a + 1], scale=-1.0,
                                                    accum_out=rowsum[:, hh, a:a + 1])
                    last.then_inc(exp_done.sem, 1)

                def take_probs(hh):
                    n = at * NH + hh
                    act.wait_ge(pt_full.sem, pt_full.at(b, n + 1))
                    nc.scalar.activation(probT[:, n % 2, :], PT[n % 2][:, :], ACT.Copy).then_inc(pt_taken.sem, 1)

                for i in range(NH + 4):
                    if i < NH:
                        exponentials(i)
                    if i >= 4:
                        take_probs(i - 4)

            for tally in (g_taken["act"], pt_taken, x_out,):
                tally.prime(act)
            with act.Fori(0, BATCH) as b:
                take_T(b, "encT", encT, None, None)
                root(b, 0)
                take_T(b, "hT1", hT, "ln1_s", "ln1_b")
                take_T(b, "k", kT, None, "b_k1")
                attend(b, 0)
                take_T(b, "xk", kT, None, "b_k2")
                root(b, 1)
                take_T(b, "hT2", hT, "ln2_s", "ln2_b")
                attend(b, 1)
                root(b, 2)
                take_T(b, "hT3", hT, "ln3_s", "ln3_b")
                for i in range(2 * FQ):
                    n = first_g["f1"] + i
                    quarter, k = i // 2, i % 2
                    act.wait_ge(g_full.sem, g_full.at(b, n + 1))
                    for m in range(2):
                        last = nc.scalar.activation(f1T[:, quarter % 2, 2 * k + m, :],
                                                    G[n % 2][:, m * SEQ:(m + 1) * SEQ], ACT.Gelu_apprx_tanh,
                                                    bias=b1_col[:, 2 * i + m:2 * i + m + 1])
                    last.then_inc(g_taken["act"].sem, 1)
                act.wait_ge(o_taken.sem, o_taken.at(b, 2 * CG + TT))
                act.dma_start(x3_dram[b, :, :].rearrange("(a p) n -> p a n", p=P),
                              x[:, :].rearrange("p (a n) -> p a n", a=TT)).then_inc(x_out.sem, 16)
            act.wait_ge(x_out.sem, x_out.at(BATCH - 1, 1))


def vectors(T):
    T["b_q1"], T["b_k1"], T["b_v1"] = (T["b_qkv"][i * DM:(i + 1) * DM] for i in range(3))
    T["b_k2"], T["b_v2"] = (T["b_kv"][i * DM:(i + 1) * DM] for i in range(2))
    T["vecs_a"] = ["b_q1", "b_k1", "b_v1", "b_q", "b_k2", "b_v2", "ln1_s", "ln1_b", "ln2_s", "ln2_b", "ln3_s", "ln3_b"]


N_HEADS, HS = 32, 16
MIX = 5
MIX_RANK = 32
DECAY_RANK = 64
IQ, JP = 4, 2
IROWS, JCOLS = HS // IQ, 2
STEPS = IQ * JP
JOWN = 4


def vectors_b(T):
    for f in range(MIX):
        T[f"stack{f}"] = T["maa_stack"][0, f, :]
    T["u_flat"] = T["u"].rearrange("h s a -> (h s a)")
    T["vecs_b"] = ["m_ln1_w", "m_ln1_b", "m_ln2_w", "m_ln2_b", "maa_x", "time_decay", "u_flat", "gn_w", "gn_b",
                   "ffn_maa_k", "ffn_maa_r"] + [f"stack{f}" for f in range(MIX)]


def recurrent_block(nc, sems, T, x3_dram, out_dram):
    with ExitStack() as ctx:
        def sb(name, *shape):
            return ctx.enter_context(nc.sbuf_tensor("b_" + name, list(shape), F32))

        def sem(name):
            return sems.enter_context(nc.semaphore("b_" + name))

        def dram(name, *shape):
            return nc.dram_tensor("b_" + name, list(shape), F32, kind="Internal").ap()

        w_dram = dram("w_all", BATCH, DM, SEQ + 1)
        k_dram, v_dram, r_dram, g_dram, bv_dram, o_dram = (
            dram(n, BATCH, DM, SEQ) for n in ("k_all", "v_all", "r_all", "g_all", "bv_all", "o_all"))

        W = {n: sb(n, P, CG, DM) for n in ("Wk", "Wv", "Wr", "Wg", "Wo", "Wfr", "Wfk", "Wfv")}
        maa_w1 = sb("maa_w1", P, CG, 2 * P)
        maa_w2 = sb("maa_w2", P, 2, DM)
        td_w1 = sb("td_w1", P, CG, P)
        td_w2 = sb("td_w2", P, DM)
        vec = sb("vec", P, len(T["vecs_b"]), CG)
        ident = sb("ident", P, P)
        same_head = sb("same_head", P, P)
        mean_head = sb("mean_head", P, P)
        f_row = sb("f_row", P, MIX - 1)
        eps_col = sb("eps_col", P, 1)
        state_rows = sb("state_rows", 2 * BATCH, DM)
        stateT = sb("stateT", P, CG, 2 * BATCH)
        xa = sb("xa", P, TT, DM)
        xaT = sb("xaT", P, CG, SEQ + 1)
        sx = sb("sx", P, CG, SEQ)
        mixed = sb("mixed", P, 2, CG, SEQ)
        t1 = sb("t1", P, 2, SEQ)
        t1f = sb("t1f", P, 2, SEQ)
        tdt = sb("tdt", P, SEQ)
        kT, vT, rT, gT = (sb(n, P, CG, SEQ) for n in ("kT", "vT", "rT", "gT"))
        wT = sb("wT", P, CG, SEQ + 1)
        stats = sb("stats", P, 2, TT, 6)
        meanvar = sb("meanvar", P, 2, TT, 2)
        std = sb("std", P, 2, TT)
        rstd = sb("rstd", P, 2, TT)
        ws = sb("ws", P, 2, IROWS, SEQ + 1)
        ks = sb("ks", P, 2, IROWS, SEQ)
        rs = sb("rs", P, 2, IROWS, SEQ)
        vs = sb("vs", P, JOWN, SEQ)
        s0 = sb("s0", P, HS, JOWN)
        ring = sb("ring", P, 2, JCOLS, IROWS, SEQ + 1)
        part = sb("part", P, JCOLS, SEQ)
        osum = sb("osum", P, JOWN, SEQ)
        o = sb("o", P, CG, SEQ)
        bv = sb("bv", P, CG, SEQ)
        g = sb("g", P, CG, SEQ)
        xr = sb("xr", P, TT, DM)
        sq = sb("sq", P, CG, SEQ)
        xcT = sb("xcT", P, CG, SEQ + 1)
        sx2 = sb("sx2", P, CG, SEQ)

        def psum(name):
            return ctx.enter_context(nc.psum_tensor("b_" + name, [P, 512], F32))

        RING = 4
        BANKS = {"a": [psum(f"A{i}") for i in range(RING)], "c": [psum(f"C{i}") for i in range(RING)]}
        TILES = {
            "a": [("xaT", "act")] * 2 + [("t1", "act"), None] + [("mix0", "dve")] * 2 + [("mix1", "dve")] * 2
            + [("k", "act")] * 2 + [("mix2", "dve")] * 2 + [("td1", "act"), None] + [("mix3", "dve")] * 2
            + [("td2", "act")] * 2 + [("v", "act")] * 2 + [("mix4", "dve")] * 2 + [("r", "act")] * 2
            + [("g", "dve")] * 2 + [("bonus", "dve")] * 2,
            "c": [("mean", "dve")] * 2 + [("var", "act")] * 2 + [("wo", "dve")] * 2 + [("xcT", "act")] * 2
            + [("rr", "act")] * 2 + [("kk", "act")] * 2 + [("kv", "dve")] * 2 + [None] * 2,
        }
        first, full, taken = {}, {}, {}
        for part_name, tiles in TILES.items():
            assert len(tiles) % RING == 0
            for n, t in enumerate(tiles):
                if t:
                    first.setdefault(t[0], (part_name, n))
            full[part_name] = Tally(sem(f"{part_name}_full"), sum(t is not None for t in tiles), by="pe")
            taken[part_name] = {e: Tally(sem(f"{part_name}_taken_{e}"), sum(t is not None and t[1] == e for t in tiles),
                                         by=e)
                                for e in ("act", "dve")}

        def tile(name, k):
            which, n = first[name]
            return BANKS[which][(n + k) % RING]

        def upto(which, n, who):
            return sum(t is not None and who in (None, t[1]) for t in TILES[which][:n + 1])

        def filled(b, name, k):
            which, n = first[name]
            return full[which].sem, full[which].at(b, upto(which, n + k, None))

        def emptied(b, name, k):
            which, n = first[name]
            t = taken[which][TILES[which][n + k][1]]
            return t.sem, t.at(b, upto(which, n + k, TILES[which][n + k][1]))

        def bank_free(b, name, k):
            which, n = first[name]
            m = n + k - RING
            while TILES[which][m] is None:
                m -= RING
            t = taken[which][TILES[which][m][1]]
            return t.sem, t.at(b, upto(which, m, TILES[which][m][1]) if m >= 0 else 0)

        def full_sem(name):
            return full[first[name][0]].sem

        def empty_sem(name):
            which, n = first[name]
            return taken[which][TILES[which][n][1]].sem

        weights_in = sem("weights_in")
        pads_made = sem("pads_made")
        consts_made = sem("consts_made")
        state_turned = sem("state_turned")
        state_kept = sem("state_kept")
        xa_in = Tally(sem("xa_in"), 1, 16)
        a_var = Tally(sem("a_var"), 1)
        a_std = Tally(sem("a_std"), 1)
        a_h = Tally(sem("a_h"), 1, by="dve")
        sx_made = Tally(sem("sx_made"), 1)
        z_made = Tally(sem("z_made"), 1)
        f_made = Tally(sem("f_made"), MIX - 1)
        mix_made = Tally(sem("mix_made"), MIX)
        e_made = Tally(sem("e_made"), 2)
        w_made = Tally(sem("w_made"), 1)
        kwvr_out = Tally(sem("kwvr_out"), 4, 16, by="act")
        tanh_g = Tally(sem("tanh_g"), 2)
        rku_made = Tally(sem("rku_made"), 2)
        g_out = Tally(sem("g_out"), 1, 16, by="sp")
        bv_out = Tally(sem("bv_out"), 1, 16, by="sp")
        wkr_in = [Tally(sem(f"wkr_in{i}"), IQ // 2, 48) for i in range(2)]
        vs_in = Tally(sem("vs_in"), 1, 80)
        kv_made = Tally(sem("kv_made"), STEPS, by="pool")
        scanned = Tally(sem("scanned"), STEPS)
        weighed = Tally(sem("weighed"), STEPS, by="dve")
        reduced = Tally(sem("reduced"), STEPS, by="dve")
        summed = Tally(sem("summed"), STEPS - JP)
        o_out = Tally(sem("o_out"), 1, 16, by="sp")
        c_in = Tally(sem("c_in"), 4, 16)
        o_made = Tally(sem("o_made"), 1)
        sq_made = Tally(sem("sq_made"), 1)
        rstd_made = Tally(sem("rstd_made"), 1)
        y_made = Tally(sem("y_made"), 1)
        yn_made = Tally(sem("yn_made"), 1)
        yg_made = Tally(sem("yg_made"), 1)
        c_var = Tally(sem("c_var"), 1)
        c_std = Tally(sem("c_std"), 1)
        c_h = Tally(sem("c_h"), 1)
        sx2_made = Tally(sem("sx2_made"), 1)
        xk_made = Tally(sem("xk_made"), 1)
        xr_made = Tally(sem("xr_made"), 1)
        kk_made = Tally(sem("kk_made"), 1)
        rr_made = Tally(sem("rr_made"), 1)
        rkv_made = Tally(sem("rkv_made"), 1)
        out_made = Tally(sem("out_made"), 1)
        out_out = Tally(sem("out_out"), 1, 16, by="sp")
        a_links = Tally(sem("a_links"), TT + 1)
        c_links = Tally(sem("c_links"), TT + 1)
        relu_made = Tally(sem("relu_made"), 1)

        vi = {name: i for i, name in enumerate(T["vecs_b"])}

        def col(name, c):
            return vec[:, vi[name], c:c + 1]

        def alone(eng):
            eng.nop(nofuse=True)

        def pipeline(eng, body):
            body(0, None, None)
            body(1, 0, None)
            with eng.Fori(0, BATCH - 2) as i:
                body(i + 2, i + 1, i)
            body(None, BATCH - 1, BATCH - 2)
            body(None, None, BATCH - 1)

        def flat(ap):
            return ap.rearrange("p c t -> p (c t)")

        block = ctx.enter_context(nc.Block())
        N_DMAS = 8 + 5 + len(vi) + 1

        @block.sync
        def _(sp):
            with nc.allow_non_contiguous_dma(reason="channel vectors, once"):
                for name, i in vi.items():
                    sp.dma_start(vec[:, i, :], T[name].rearrange("(c p) -> p c", p=P)).then_inc(weights_in, 16)
            sp.dma_start(state_rows[:, :], T["enc"][:, 0:2, :]).then_inc(weights_in, 16)
            sp.wait_ge(pads_made, 4)
            sp.dma_start(maa_w1[:, :, 0:MIX * MIX_RANK], T["maa_w1"].rearrange("(c p) n -> p c n", p=P))\
                .then_inc(weights_in, 16)
            sp.dma_start(maa_w2[:, 0, :], T["maa_w2"][0:4, :, :].rearrange("f d n -> (f d) n")).then_inc(weights_in, 16)
            sp.dma_start(maa_w2[0:MIX_RANK, 1, :], T["maa_w2"][4, :, :]).then_inc(weights_in, 16)
            sp.dma_start(td_w1[:, :, 0:DECAY_RANK], T["td_w1"].rearrange("(c p) n -> p c n", p=P))\
                .then_inc(weights_in, 16)
            sp.dma_start(td_w2[0:DECAY_RANK, :], T["td_w2"]).then_inc(weights_in, 16)
            sp.dma_start(W["Wk"][:, :, :], T["Wk"].rearrange("(c p) n -> p c n", p=P)).then_inc(weights_in, 16)
            for n in ("Wv", "Wr", "Wg", "Wo", "Wfr", "Wfk", "Wfv"):
                sp.dma_start(W[n][:, :, :], T[n].rearrange("(c p) n -> p c n", p=P)).then_inc(weights_in, 16)

            def wkr(s, q):
                for tile_, dram_ in ((ws, w_dram), (ks, k_dram), (rs, r_dram)):
                    n = tile_.shape[-1]
                    rows = dram_[s, :, :].rearrange("(h q i) t -> h q (i t)", q=IQ, i=IROWS)[:, q:q + 1, :]
                    sp.dma_start(tile_[:, q % 2, :, :].rearrange("p i t -> p (i t)"),
                                 rows.to_broadcast([N_HEADS, P // N_HEADS, IROWS * n]))\
                        .then_inc(wkr_in[q % 2].sem, 16)

            def body(a, s, c):
                if a is not None:
                    sp.wait_ge(a_h.sem, a_h.at(a, 0))
                    alone(sp)
                    sp.wait_ge(full["a"].sem, full["a"].at(a, 0))
                    alone(sp)
                    sp.dma_start(xa[:, :, :], x3_dram[a, :, :].rearrange("(a p) n -> p a n", p=P))\
                        .then_inc(xa_in.sem, 16)
                if s is not None:
                    sp.wait_ge(kwvr_out.sem, kwvr_out.at(s + 1, 0))
                    alone(sp)
                    sp.wait_ge(kv_made.sem, kv_made.at(s, 0))
                    alone(sp)
                    sp.dma_start(vs[:, :, :], v_dram[s, :, :].rearrange("(p j) t -> p j t", j=JOWN))\
                        .then_inc(vs_in.sem, 16)
                    starts = T["enc"][s, 2:2 + HS, :].rearrange("r (q i g j) -> (r q) g i j", q=DM // (HS * HS), i=HS,
                                                                j=JOWN)
                    for quad in range(P // N_HEADS):
                        sp.dma_start(s0[quad:P:P // N_HEADS, :, :], starts[:, quad, :, :]).then_inc(vs_in.sem, 16)
                    sp.wait_ge(weighed.sem, weighed.at(s, 0))
                    alone(sp)
                    wkr(s, 0)
                    wkr(s, 1)
                if c is not None:
                    sp.wait_ge(bv_out.sem, bv_out.at(c + 1, 0))
                    alone(sp)
                    sp.wait_ge(g_out.sem, g_out.at(c + 1, 0))
                    alone(sp)
                    sp.wait_ge(o_out.sem, o_out.at(c + 1, 0))
                    alone(sp)
                    sp.wait_ge(out_out.sem, out_out.at(c, 0))
                    alone(sp)
                    for t, d in ((o, o_dram), (bv, bv_dram), (g, g_dram)):
                        sp.dma_start(t[:, :, :], d[c, :, :].rearrange("(c p) t -> p c t", p=P)).then_inc(c_in.sem, 16)
                    sp.dma_start(xr[:, :, :], x3_dram[c, :, :].rearrange("(a p) n -> p a n", p=P)).then_inc(c_in.sem, 16)
                if s is not None:
                    for q in range(2, IQ):
                        sp.wait_ge(weighed.sem, weighed.at(s, 2 * (q - 1)))
                        alone(sp)
                        wkr(s, q)
                if c is not None:
                    sp.wait_ge(out_made.sem, out_made.at(c, 1))
                    alone(sp)
                    sp.dma_start(out_dram[c, :, :].rearrange("(a p) n -> p a n", p=P), xr[:, :, :])\
                        .then_inc(out_out.sem, 16)
                if a is not None:
                    sp.wait_ge(*emptied(a, "g", 1))
                    alone(sp)
                    sp.dma_start(g_dram[a, :, :].rearrange("(c p) t -> p c t", p=P), gT[:, :, :]).then_inc(g_out.sem, 16)
                if s is not None:
                    sp.wait_ge(summed.sem, summed.at(s, STEPS - JP))
                    alone(sp)
                    sp.dma_start(o_dram[s, :, :].rearrange("(p j) t -> p j t", j=JOWN), osum[:, :, :])\
                        .then_inc(o_out.sem, 16)
                if a is not None:
                    sp.wait_ge(*emptied(a, "bonus", 1))
                    alone(sp)
                    sp.dma_start(bv_dram[a, :, :].rearrange("(c p) t -> p c t", p=P), mixed[:, 0, :, :])\
                        .then_inc(bv_out.sem, 16)

            for tally in (bv_out, g_out, o_out, out_out,):
                tally.prime(sp)
            pipeline(sp, body)
            sp.wait_ge(out_out.sem, out_out.at(BATCH - 1, 1))

        @block.gpsimd
        def _(pool):
            for t in (maa_w1[:, :, :], maa_w2[:, :, :], td_w1[:, :, :], td_w2[:, :]):
                nc.gpsimd.memset(t, 0.0).then_inc(pads_made, 1)
            nc.gpsimd.memset(ident[:, :], 0.0)
            nc.gpsimd.memset(eps_col[:, :], EPS)
            nc.gpsimd.memset(wT[:, :, 0:1], 0.0)
            nc.gpsimd.memset(same_head[:, :], 1.0)
            nc.gpsimd.memset(mean_head[:, :], 1.0 / HS)
            nc.gpsimd.memset(f_row[:, :], 1.0).then_inc(consts_made, 1)
            pool.wait_ge(consts_made, 1)
            nc.gpsimd.affine_select(out=ident[:, :], in_=ident[:, :], compare_op=ALU.not_equal, fill=1.0, base=0,
                                    pattern=[[-1, P]], channel_multiplier=1)
            blocks = ((same_head, HS, P // HS, HS), (mean_head, HS, P // HS, HS), (f_row, MIX_RANK, MIX - 1, 1))
            for t, size, n, width in blocks:
                v_ = t[:, :].rearrange("p (n w) -> p n w", w=width)
                last = nc.gpsimd.affine_select(out=v_, in_=v_, compare_op=ALU.is_ge, fill=0.0, base=0,
                                               pattern=[[-size, n], [0, width]], channel_multiplier=1)
            last.then_inc(consts_made, 1)
            pool.wait_ge(consts_made, 2)
            for t, size, n, width in blocks:
                v_ = t[:, :].rearrange("p (n w) -> p n w", w=width)
                last = nc.gpsimd.affine_select(out=v_, in_=v_, compare_op=ALU.is_ge, fill=0.0, base=size - 1,
                                               pattern=[[size, n], [0, width]], channel_multiplier=-1)
            last.then_inc(consts_made, 1)

            def outer(s, u):
                q, jp = u // JP, u % JP
                if u == 0:
                    pool.wait_ge(vs_in.sem, vs_in.at(s, 1))
                    alone(pool)
                if jp == 0:
                    pool.wait_ge(wkr_in[q % 2].sem, wkr_in[q % 2].at(s, q // 2 + 1))
                    alone(pool)
                pool.wait_ge(reduced.sem, reduced.at(s, max(u - 1, 0)))
                alone(pool)
                slot = ring[:, u % 2, :, :, :]
                for j in range(JCOLS):
                    nc.gpsimd.tensor_copy(slot[:, j, :, 0:1],
                                          s0[:, q * IROWS:(q + 1) * IROWS, jp * JCOLS + j:jp * JCOLS + j + 1])
                nc.gpsimd.tensor_tensor(slot[:, :, :, 1:SEQ + 1],
                                        ks[:, q % 2, :, :].unsqueeze(1).to_broadcast([P, JCOLS, IROWS, SEQ]),
                                        vs[:, jp * JCOLS:(jp + 1) * JCOLS, :].unsqueeze(2)
                                        .to_broadcast([P, JCOLS, IROWS, SEQ]), ALU.mult).then_inc(kv_made.sem, 1)

            def add_xa(a, f):
                pool.wait_ge(*emptied(a, f"mix{f}", 1))
                alone(pool)
                nc.gpsimd.tensor_tensor(mixed[:, f % 2, :, :], mixed[:, f % 2, :, :], xaT[:, :, 1:SEQ + 1], ALU.add)\
                    .then_inc(mix_made.sem, 1)

            def body(a, s, c):
                if c is not None:
                    pool.wait_ge(c_in.sem, c_in.at(c, 4))
                    alone(pool)
                    nc.gpsimd.tensor_tensor(o[:, :, :], o[:, :, :], bv[:, :, :], ALU.add).then_inc(o_made.sem, 1)
                if s is not None:
                    outer(s, 0)
                if a is not None:
                    pool.wait_ge(*emptied(a, "xaT", 1))
                    alone(pool)
                    nc.gpsimd.tensor_tensor(sx[:, :, :], xaT[:, :, 0:SEQ], xaT[:, :, 1:SEQ + 1], ALU.subtract)\
                        .then_inc(sx_made.sem, 1)
                if s is not None:
                    outer(s, 1)
                if c is not None:
                    pool.wait_ge(rstd_made.sem, rstd_made.at(c, 1))
                    alone(pool)
                    nc.gpsimd.tensor_tensor(o[:, :, :], o[:, :, :], sq[:, :, :], ALU.mult).then_inc(y_made.sem, 1)
                if s is not None:
                    outer(s, 2)
                if a is not None:
                    add_xa(a, 0)
                if s is not None:
                    outer(s, 3)
                if a is not None:
                    add_xa(a, 1)
                if c is not None:
                    pool.wait_ge(*emptied(c, "xcT", 1))
                    alone(pool)
                    nc.gpsimd.tensor_tensor(sx2[:, :, :], xcT[:, :, 0:SEQ], xcT[:, :, 1:SEQ + 1], ALU.subtract)\
                        .then_inc(sx2_made.sem, 1)
                for u, f in ((4, 2), (5, 3), (6, 4)):
                    if s is not None:
                        outer(s, u)
                    if a is not None:
                        add_xa(a, f)
                if s is not None:
                    outer(s, 7)

            for tally in (kv_made,):
                tally.prime(pool)
            pipeline(pool, body)

        @block.tensor
        def _(pe):
            pe.wait_ge(weights_in, 16 * N_DMAS)
            pe.wait_ge(consts_made, 3)
            for c in range(CG):
                last = nc.tensor.transpose(BANKS["a"][0][:, c * 2 * BATCH:(c + 1) * 2 * BATCH],
                                           state_rows[:, c * P:(c + 1) * P], ident[0:2 * BATCH, 0:2 * BATCH])
            last.then_inc(state_turned, 1)
            pe.wait_ge(state_kept, 1)

            def turn(b, name, src):
                for k in range(2):
                    pe.wait_ge(*bank_free(b, name, k))
                    for m in range(2):
                        for a in range(TT):
                            c = 2 * k + m
                            last = nc.tensor.transpose(tile(name, k)[:, m * SEQ + a * P:m * SEQ + (a + 1) * P],
                                                       src[:, a, c * P:(c + 1) * P], ident[:, :])
                    last.then_inc(full_sem(name), 1)

            def project_T(b, name, w, act):
                for k in range(2):
                    pe.wait_ge(*bank_free(b, name, k))
                    for m in range(2):
                        for c in range(CG):
                            last = nc.tensor.matmul(tile(name, k)[:, m * SEQ:(m + 1) * SEQ],
                                                    w[:, c, (2 * k + m) * P:(2 * k + m + 1) * P], act[:, c, :],
                                                    start=(c == 0), stop=(c == CG - 1))
                    last.then_inc(full_sem(name), 1)

            def project(b, name, w, act):
                for a in range(TT):
                    pe.wait_ge(*bank_free(b, name, a))
                    for c in range(CG):
                        last = nc.tensor.matmul(tile(name, a)[:, :], act[:, c, a * P:(a + 1) * P], w[:, c, :],
                                                start=(c == 0), stop=(c == CG - 1))
                    last.then_inc(full_sem(name), 1)

            def by_group(b, name, weight_of, act_of):
                for k in range(2):
                    pe.wait_ge(*bank_free(b, name, k))
                    for m in range(2):
                        last = nc.tensor.matmul(tile(name, k)[:, m * SEQ:(m + 1) * SEQ], weight_of(2 * k + m),
                                                act_of(2 * k + m), start=True, stop=True)
                    last.then_inc(full_sem(name), 1)

            def mix(a, f):
                if f < MIX - 1:
                    pe.wait_ge(f_made.sem, f_made.at(a, f + 1))
                by_group(a, f"mix{f}", lambda c: maa_w2[:, f // 4, c * P:(c + 1) * P],
                         lambda c: t1f[:, f % 2, :] if f < MIX - 1 else t1[:, 1, :])

            def body(a, s, c):
                if c is not None:
                    pe.wait_ge(o_made.sem, o_made.at(c, 1))
                    by_group(c, "mean", lambda cg: mean_head[:, :], lambda cg: o[:, cg, :])
                if a is not None:
                    pe.wait_ge(a_h.sem, a_h.at(a, 1))
                    turn(a, "xaT", xa)
                if c is not None:
                    pe.wait_ge(sq_made.sem, sq_made.at(c, 1))
                    by_group(c, "var", lambda cg: mean_head[:, :], lambda cg: sq[:, cg, :])
                if a is not None:
                    pe.wait_ge(z_made.sem, z_made.at(a, 1))
                    pe.wait_ge(*bank_free(a, "t1", 0))
                    for m in range(2):
                        for cg in range(CG):
                            last = nc.tensor.matmul(tile("t1", 0)[:, m * SEQ:(m + 1) * SEQ],
                                                    maa_w1[:, cg, m * P:(m + 1) * P], mixed[:, 1, cg, :],
                                                    start=(cg == 0), stop=(cg == CG - 1))
                    last.then_inc(full["a"].sem, 1)
                if c is not None:
                    pe.wait_ge(yg_made.sem, yg_made.at(c, 1))
                    project(c, "wo", W["Wo"], o)
                if a is not None:
                    mix(a, 0)
                if c is not None:
                    pe.wait_ge(c_h.sem, c_h.at(c, 1))
                    turn(c, "xcT", sq[:, :, :].rearrange("p c t -> p (c t)").rearrange("p (a n) -> p a n", a=TT))
                if a is not None:
                    mix(a, 1)
                    pe.wait_ge(mix_made.sem, mix_made.at(a, 1))
                    project_T(a, "k", W["Wk"], mixed[:, 0, :, :])
                if c is not None:
                    pe.wait_ge(xr_made.sem, xr_made.at(c, 1))
                    project(c, "rr", W["Wfr"], g)
                    project_T(c, "kk", W["Wfk"], bv)
                if a is not None:
                    mix(a, 2)
                    pe.wait_ge(mix_made.sem, mix_made.at(a, 2))
                    pe.wait_ge(*bank_free(a, "td1", 0))
                    for cg in range(CG):
                        last = nc.tensor.matmul(tile("td1", 0)[:, 0:SEQ], td_w1[:, cg, :], mixed[:, 1, cg, :],
                                                start=(cg == 0), stop=(cg == CG - 1))
                    last.then_inc(full["a"].sem, 1)
                if c is not None:
                    pe.wait_ge(kk_made.sem, kk_made.at(c, 1))
                    project(c, "kv", W["Wfv"], sq)
                if a is not None:
                    mix(a, 3)
                    pe.wait_ge(*emptied(a, "td1", 0))
                    by_group(a, "td2", lambda cg: td_w2[:, cg * P:(cg + 1) * P], lambda cg: tdt[:, :])
                    pe.wait_ge(mix_made.sem, mix_made.at(a, 3))
                    project_T(a, "v", W["Wv"], mixed[:, 0, :, :])
                    mix(a, 4)
                    pe.wait_ge(mix_made.sem, mix_made.at(a, 4))
                    project_T(a, "r", W["Wr"], mixed[:, 1, :, :])
                    pe.wait_ge(mix_made.sem, mix_made.at(a, 5))
                    project_T(a, "g", W["Wg"], mixed[:, 0, :, :])
                    pe.wait_ge(rku_made.sem, rku_made.at(a, 2))
                    by_group(a, "bonus", lambda cg: same_head[:, :], lambda cg: mixed[:, 1, cg, :])

            for tally in (full["a"], full["c"],):
                tally.prime(pe)
            pipeline(pe, body)

        @block.vector
        def _(dve):
            dve.wait_ge(weights_in, 16 * N_DMAS)
            dve.wait_ge(consts_made, 3)
            dve.wait_ge(state_turned, 1)
            nc.vector.tensor_copy(stateT[:, :, :].rearrange("p c b -> p (c b)"),
                                  BANKS["a"][0][:, 0:CG * 2 * BATCH]).then_inc(state_kept, 1)

            def layernorm(b, i, src, dst, links, var_made, std_made, h_made):
                for a in range(TT):
                    nc.vector.bn_stats(stats[:, i, a, :], src[:, a, :]).then_inc(links.sem, 1)
                dve.wait_ge(links.sem, links.at(b, TT))
                alone(dve)
                for a in range(TT):
                    last = nc.vector.bn_aggr(meanvar[:, i, a, :], stats[:, i, a, :])
                last.then_inc(var_made.sem, 1)
                dve.wait_ge(std_made.sem, std_made.at(b, 1))
                nc.vector.reciprocal(rstd[:, i, :], std[:, i, :]).then_inc(links.sem, 1)
                dve.wait_ge(links.sem, links.at(b, TT + 1))
                for a in range(TT):
                    last = nc.vector.tensor_scalar(dst[:, a, :], src[:, a, :], meanvar[:, i, a, 0:1], rstd[:, i, a:a + 1],
                                                   ALU.subtract, ALU.mult)
                last.then_inc(h_made.sem, 1)

            def step(s, u):
                q, jp = u // JP, u % JP
                slot = ring[:, u % 2, :, :, :]
                dve.wait_ge(kv_made.sem, kv_made.at(s, u + 1))
                if jp == 0:
                    dve.wait_ge(wkr_in[q % 2].sem, wkr_in[q % 2].at(s, q // 2 + 1))
                alone(dve)
                decay = flat(ws[:, q % 2, :, :])
                for j in range(JCOLS):
                    x_ = flat(slot[:, j, :, :])
                    last = nc.vector.tensor_tensor_scan(x_, decay, x_, 0.0, ALU.mult, ALU.add)
                last.then_inc(scanned.sem, 1)
                dve.wait_ge(scanned.sem, scanned.at(s, u + 1))
                x_ = slot[:, :, :, 0:SEQ]
                nc.vector.tensor_tensor(x_, x_, rs[:, q % 2, :, :].unsqueeze(1).to_broadcast([P, JCOLS, IROWS, SEQ]),
                                        ALU.mult).then_inc(weighed.sem, 1)
                dve.wait_ge(weighed.sem, weighed.at(s, u + 1))
                if u == 0:
                    dve.wait_ge(o_out.sem, o_out.at(s, 0))
                dst = osum[:, jp * JCOLS:(jp + 1) * JCOLS, :]
                to = dst if q == 0 else part[:, :, :]
                nc.vector.tensor_reduce(to, x_.rearrange("p j i t -> p j t i"), AX_X, ALU.add).then_inc(reduced.sem, 1)
                if q:
                    dve.wait_ge(reduced.sem, reduced.at(s, u + 1))
                    nc.vector.tensor_tensor(dst, dst, part[:, :, :], ALU.add).then_inc(summed.sem, 1)

            def shift(a, f):
                for k in range(2):
                    dve.wait_ge(*filled(a, f"mix{f}", k))
                    if f == 0 and k == 0:
                        dve.wait_ge(bv_out.sem, bv_out.at(a, 0))
                    for m in range(2):
                        c = 2 * k + m
                        last = nc.vector.scalar_tensor_tensor(out=mixed[:, f % 2, c, :],
                                                              in0=tile(f"mix{f}", k)[:, m * SEQ:(m + 1) * SEQ],
                                                              scalar=col(f"stack{f}", c), in1=sx[:, c, :],
                                                              op0=ALU.add, op1=ALU.mult)
                    last.then_inc(empty_sem(f"mix{f}"), 1)

            def body(a, s, c):
                if c is not None:
                    for k in range(2):
                        dve.wait_ge(*filled(c, "mean", k))
                        x_ = flat(o[:, 2 * k:2 * k + 2, :])
                        nc.vector.tensor_tensor(x_, x_, tile("mean", k)[:, :], ALU.subtract).then_inc(empty_sem("mean"), 1)
                if a is not None:
                    dve.wait_ge(xa_in.sem, xa_in.at(a, 1))
                    layernorm(a, 0, xa, xa, a_links, a_var, a_std, a_h)
                if s is not None:
                    step(s, 0)
                if c is not None:
                    dve.wait_ge(*emptied(c, "var", 1))
                    nc.vector.reciprocal(sq[:, :, :], sq[:, :, :]).then_inc(rstd_made.sem, 1)
                if a is not None:
                    dve.wait_ge(sx_made.sem, sx_made.at(a, 1))
                    for cg in range(CG):
                        last = nc.vector.scalar_tensor_tensor(out=mixed[:, 1, cg, :], in0=sx[:, cg, :],
                                                              scalar=col("maa_x", cg), in1=xaT[:, cg, 1:SEQ + 1],
                                                              op0=ALU.mult, op1=ALU.add)
                    last.then_inc(z_made.sem, 1)
                if s is not None:
                    step(s, 1)
                if c is not None:
                    dve.wait_ge(yn_made.sem, yn_made.at(c, 1))
                    nc.vector.scalar_tensor_tensor(out=flat(o[:, :, :]), in0=flat(o[:, :, :]), scalar=0.5,
                                                   in1=flat(g[:, :, :]), op0=ALU.mult, op1=ALU.mult)\
                        .then_inc(yg_made.sem, 1)
                if a is not None:
                    dve.wait_ge(*emptied(a, "t1", 0))
                    for f in range(2):
                        nc.vector.tensor_scalar(t1f[:, f, :], t1[:, 0, :], f_row[:, f:f + 1], None, ALU.mult)\
                            .then_inc(f_made.sem, 1)
                    shift(a, 0)
                    nc.vector.tensor_scalar(t1f[:, 0, :], t1[:, 0, :], f_row[:, 2:3], None, ALU.mult)\
                        .then_inc(f_made.sem, 1)
                if c is not None:
                    for k in range(TT):
                        dve.wait_ge(*filled(c, "wo", k))
                        nc.vector.tensor_tensor(xr[:, k, :], tile("wo", k)[:, :], xr[:, k, :], ALU.add).then_inc(empty_sem("wo"), 1)
                    dve.wait_ge(*emptied(c, "wo", 1))
                    h2 = flat(sq[:, :, :]).rearrange("p (a n) -> p a n", a=TT)
                    layernorm(c, 1, xr, h2, c_links, c_var, c_std, c_h)
                if s is not None:
                    step(s, 2)
                if a is not None:
                    shift(a, 1)
                    nc.vector.tensor_scalar(t1f[:, 1, :], t1[:, 0, :], f_row[:, 3:4], None, ALU.mult)\
                        .then_inc(f_made.sem, 1)
                if s is not None:
                    step(s, 3)
                if c is not None:
                    dve.wait_ge(sx2_made.sem, sx2_made.at(c, 1))
                    for cg in range(CG):
                        last = nc.vector.scalar_tensor_tensor(out=g[:, cg, :], in0=sx2[:, cg, :],
                                                              scalar=col("ffn_maa_r", cg), in1=xcT[:, cg, 1:SEQ + 1],
                                                              op0=ALU.mult, op1=ALU.add)
                    for cg in range(CG):
                        last = nc.vector.scalar_tensor_tensor(out=bv[:, cg, :], in0=sx2[:, cg, :],
                                                              scalar=col("ffn_maa_k", cg), in1=xcT[:, cg, 1:SEQ + 1],
                                                              op0=ALU.mult, op1=ALU.add)
                    last.then_inc(xr_made.sem, 1)
                if a is not None:
                    shift(a, 2)
                if s is not None:
                    step(s, 4)
                if a is not None:
                    shift(a, 3)
                if c is not None:
                    dve.wait_ge(*emptied(c, "rr", 1))
                    nc.vector.tensor_scalar(o[:, :, :], o[:, :, :], 0.5, 0.5, ALU.mult, ALU.add).then_inc(rr_made.sem, 1)
                    dve.wait_ge(rr_made.sem, rr_made.at(c, 1))
                    for k in range(TT):
                        dve.wait_ge(*filled(c, "kv", k))
                        x_ = flat(o[:, 2 * k:2 * k + 2, :])
                        nc.vector.tensor_tensor(x_, x_, tile("kv", k)[:, :], ALU.mult).then_inc(empty_sem("kv"), 1)
                    dve.wait_ge(*emptied(c, "kv", 1))
                    nc.vector.tensor_tensor(xr[:, :, :].rearrange("p a n -> p (a n)"),
                                            xr[:, :, :].rearrange("p a n -> p (a n)"), flat(o[:, :, :]), ALU.add)\
                        .then_inc(out_made.sem, 1)
                if s is not None:
                    step(s, 5)
                if a is not None:
                    shift(a, 4)
                if s is not None:
                    step(s, 6)
                if a is not None:
                    dve.wait_ge(*emptied(a, "r", 1))
                    for cg in range(CG):
                        last = nc.vector.scalar_tensor_tensor(out=mixed[:, 1, cg, :], in0=kT[:, cg, :],
                                                              scalar=col("u_flat", cg), in1=rT[:, cg, :],
                                                              op0=ALU.mult, op1=ALU.mult)
                        if cg % 2:
                            last.then_inc(rku_made.sem, 1)
                if s is not None:
                    step(s, 7)
                if a is not None:
                    for k in range(2):
                        dve.wait_ge(tanh_g.sem, tanh_g.at(a, k + 1))
                        x_ = flat(gT[:, 2 * k:2 * k + 2, :])
                        nc.vector.scalar_tensor_tensor(out=x_, in0=x_, scalar=1.0, in1=tile("g", k)[:, :],
                                                            op0=ALU.add, op1=ALU.mult).then_inc(empty_sem("g"), 1)
                    for k in range(2):
                        dve.wait_ge(*filled(a, "bonus", k))
                        nc.vector.tensor_tensor(flat(mixed[:, 0, 2 * k:2 * k + 2, :]), tile("bonus", k)[:, :],
                                                     flat(vT[:, 2 * k:2 * k + 2, :]), ALU.mult).then_inc(empty_sem("bonus"), 1)

            for tally in (taken["a"]["dve"], taken["c"]["dve"], a_h, weighed, reduced,):
                tally.prime(dve)
            pipeline(dve, body)

        @block.scalar
        def _(act):
            act.wait_ge(weights_in, 16 * N_DMAS)
            act.wait_ge(consts_made, 3)
            act.wait_ge(state_kept, 1)

            def root(b, i, var_made, std_made):
                act.wait_ge(var_made.sem, var_made.at(b, 1))
                nc.scalar.activation(std[:, i, :], meanvar[:, i, :, 1], ACT.Sqrt, bias=eps_col[:, :])\
                    .then_inc(std_made.sem, 1)

            def take_ln(b, name, dst, scale, bias, which):
                nc.scalar.copy(dst[:, :, 0:1], stateT[:, :, bass.ds(2 * b + which, 1)])
                for k in range(2):
                    act.wait_ge(*filled(b, name, k))
                    for m in range(2):
                        cg = 2 * k + m
                        last = nc.scalar.activation(dst[:, cg, 1:SEQ + 1], tile(name, k)[:, m * SEQ:(m + 1) * SEQ],
                                                    ACT.Identity, bias=col(bias, cg), scale=col(scale, cg))
                    last.then_inc(empty_sem(name), 1)

            def take(a, name, dst, dram_):
                for k in range(2):
                    act.wait_ge(*filled(a, name, k))
                    if k == 0:
                        act.wait_ge(kwvr_out.sem, kwvr_out.at(a, 0))
                    nc.scalar.activation(flat(dst[:, 2 * k:2 * k + 2, :]), tile(name, k)[:, :], ACT.Copy).then_inc(empty_sem(name), 1)
                act.wait_ge(*emptied(a, name, 1))
                alone(act)
                act.dma_start(dram_[a, :, :].rearrange("(c p) t -> p c t", p=P), dst[:, :, :])\
                    .then_inc(kwvr_out.sem, 16)

            def body(a, s, c):
                if c is not None:
                    act.wait_ge(*emptied(c, "mean", 1))
                    nc.scalar.activation(sq[:, :, :], o[:, :, :], ACT.Square).then_inc(sq_made.sem, 1)
                if a is not None:
                    root(a, 0, a_var, a_std)
                    take_ln(a, "xaT", xaT, "m_ln1_w", "m_ln1_b", 1)
                if c is not None:
                    act.wait_ge(*filled(c, "var", 1))
                    for k in range(2):
                        nc.scalar.activation(flat(sq[:, 2 * k:2 * k + 2, :]), tile("var", k)[:, :], ACT.Sqrt,
                                                  bias=eps_col[:, :]).then_inc(empty_sem("var"), 1)
                if a is not None:
                    act.wait_ge(*filled(a, "t1", 0))
                    nc.scalar.activation(t1[:, :, :], tile("t1", 0)[:, :].rearrange("p (m t) -> p m t", m=2),
                                              ACT.Tanh).then_inc(empty_sem("t1"), 1)
                if c is not None:
                    act.wait_ge(y_made.sem, y_made.at(c, 1))
                    for cg in range(CG):
                        last = nc.scalar.activation(o[:, cg, :], o[:, cg, :], ACT.Identity, bias=col("gn_b", cg),
                                                    scale=col("gn_w", cg))
                    last.then_inc(yn_made.sem, 1)
                    root(c, 1, c_var, c_std)
                    take_ln(c, "xcT", xcT, "m_ln2_w", "m_ln2_b", 0)
                if a is not None:
                    take(a, "k", kT, k_dram)
                if c is not None:
                    for k in range(TT):
                        act.wait_ge(*filled(c, "rr", k))
                        nc.scalar.activation(flat(o[:, 2 * k:2 * k + 2, :]), tile("rr", k)[:, :], ACT.Tanh,
                                                  scale=0.5).then_inc(empty_sem("rr"), 1)
                    for k in range(2):
                        act.wait_ge(*filled(c, "kk", k))
                        nc.scalar.activation(flat(sq[:, 2 * k:2 * k + 2, :]), tile("kk", k)[:, :], ACT.Relu).then_inc(empty_sem("kk"), 1)
                    act.wait_ge(*emptied(c, "kk", 1))
                    nc.scalar.activation(sq[:, :, :], sq[:, :, :], ACT.Square).then_inc(kk_made.sem, 1)
                if a is not None:
                    act.wait_ge(*filled(a, "td1", 0))
                    nc.scalar.activation(tdt[:, :], tile("td1", 0)[:, 0:SEQ], ACT.Tanh).then_inc(empty_sem("td1"), 1)
                    for k in range(2):
                        act.wait_ge(*filled(a, "td2", k))
                        for m in range(2):
                            cg = 2 * k + m
                            last = nc.scalar.activation(wT[:, cg, 1:SEQ + 1], tile("td2", k)[:, m * SEQ:(m + 1) * SEQ], ACT.Exp,
                                                        bias=col("time_decay", cg))
                        last.then_inc(empty_sem("td2"), 1)
                    act.wait_ge(*emptied(a, "td2", 1))
                    nc.scalar.activation(wT[:, :, 1:SEQ + 1], wT[:, :, 1:SEQ + 1], ACT.Exp, scale=-1.0).then_inc(w_made.sem, 1)
                    act.wait_ge(w_made.sem, w_made.at(a, 1))
                    alone(act)
                    act.dma_start(w_dram[a, :, :].rearrange("(c p) t -> p c t", p=P), wT[:, :, :])\
                        .then_inc(kwvr_out.sem, 16)
                    take(a, "v", vT, v_dram)
                    take(a, "r", rT, r_dram)
                    for k in range(2):
                        act.wait_ge(*filled(a, "g", k))
                        if k == 0:
                            act.wait_ge(g_out.sem, g_out.at(a, 0))
                        nc.scalar.activation(flat(gT[:, 2 * k:2 * k + 2, :]), tile("g", k)[:, :], ACT.Tanh, scale=0.5)\
                            .then_inc(tanh_g.sem, 1)

            for tally in (taken["a"]["act"], taken["c"]["act"], kwvr_out,):
                tally.prime(act)
            pipeline(act, body)


def two_layers(nc, T, out_dram):
    vectors(T)
    vectors_b(T)
    with ExitStack() as sems:
        x3_dram = nc.dram_tensor("x3_all", [BATCH, SEQ, DM], F32, kind="Internal").ap()
        attention_block(nc, sems, T, x3_dram)
        recurrent_block(nc, sems, T, x3_dram, out_dram)


_INPUTS = {"x": "x", "enc": "ctx_2048", "mask_self": "mask_1x1xSxS2_fc1", "mask_cross": "mask_Bx1xSxS2_ff1",
           "m_ln1_w": "L1_xattn_ln1_w", "m_ln1_b": "L1_xattn_ln1_b", "m_ln2_w": "L1_xattn_ln2_w",
           "m_ln2_b": "L1_xattn_ln2_b"}
_INPUTS |= {n: "L0_xattn_" + n for n in ("ln1_s", "ln1_b", "w_qkv", "b_qkv", "w_ao", "b_ao", "ln2_s", "ln2_b", "w_q",
                                         "b_q", "w_kv", "b_kv", "w_co", "b_co", "ln3_s", "ln3_b", "w1", "b1", "w2",
                                         "b2")}
_INPUTS |= {n: "L1_xattn_" + n for n in ("maa_x", "maa_w1", "maa_w2", "maa_stack", "time_decay", "td_w1", "td_w2", "u",
                                         "Wr", "Wk", "Wv", "Wg", "Wo", "gn_w", "gn_b", "ffn_maa_k", "ffn_maa_r", "Wfk",
                                         "Wfr", "Wfv")}
_TURNED = ("Wr", "Wk", "Wv", "Wg", "Wo", "Wfk", "Wfr", "Wfv")


def kernel(**inputs):
    import numpy as np
    import concourse.bacc as bacc
    from concourse.bass_utils import run_bass_kernel_spmd as run

    nc = bacc.Bacc("TRN2", target_bir_lowering=False, num_devices=1)
    arrays, T = {}, {}
    for name, given in _INPUTS.items():
        a = np.asarray(inputs[given])
        a = np.ascontiguousarray(a.T if name in _TURNED else a)
        arrays[f"in_{name}_dram"] = a
        T[name] = nc.dram_tensor(f"in_{name}_dram", a.shape, mybir.dt.from_np(a.dtype), kind="ExternalInput").ap()
    T["mask_self"] = T["mask_self"][0, 0, :, :]
    T["mask_cross"] = T["mask_cross"][:, 0, :, :]
    out = nc.dram_tensor("out_0_dram", (BATCH, SEQ, DM), F32, kind="ExternalOutput").ap()
    two_layers(nc, T, out)
    r = run(nc, [arrays], core_ids=[0])
    return r.results[0]["out_0_dram"]
```

```python
from contextlib import ExitStack

import concourse.bass as bass
from concourse import mybir

F32 = mybir.dt.float32
ALU = mybir.AluOpType
ACT = mybir.ActivationFunctionType
AX_X = mybir.AxisListType.X

P = 128
BATCH, SEQ, DM = 8, 256, 512
TT = SEQ // P
CG = DM // P
NH, HD = 16, 32
HPG = P // HD
FF = 4 * DM
FQ = 4
PARTS = CG
EPS = 1e-5
MASKED = 10000.0
SCORE_SCALE = float(HD) ** -0.5


class Tally:

    def __init__(self, sem, per, unit=1, by=None):
        self.sem, self.per, self.unit, self.by = sem, per, unit, by
        self.start = unit if by else 0

    def at(self, b, k):
        assert k or self.by
        return b * (self.per * self.unit) + (k * self.unit + self.start)

    def prime(self, eng):
        eng.sem_inc(self.sem, self.unit)


def attention_block(nc, sems, T, x3_dram):
    with ExitStack() as ctx:
        def sb(name, *shape):
            return ctx.enter_context(nc.sbuf_tensor("a_" + name, list(shape), F32))

        def sem(name):
            return sems.enter_context(nc.semaphore("a_" + name))

        def psum(name):
            return ctx.enter_context(nc.psum_tensor("a_" + name, [P, 512], F32))

        w_qkv = sb("w_qkv", P, CG, 3 * DM)
        w_ao = sb("w_ao", P, CG, DM)
        w_q = sb("w_q", P, CG, DM)
        w_kv = sb("w_kv", P, CG, 2 * DM)
        w_co = sb("w_co", P, CG, DM)
        ring = sb("ring", P, 2, CG * DM)
        vec = sb("vec", P, len(T["vecs_a"]), CG)
        b1_col = sb("b1_col", P, FF // P)
        head_row = sb("head_row", P, HPG)
        ident = sb("ident", P, P)
        bias_all = sb("bias_all", P, 3, DM)
        mask = sb("mask", P, 2, TT * SEQ)
        fill = sb("fill", P, 2, TT * SEQ)
        x_new = sb("x_new", P, TT * DM)
        x = sb("x", P, TT * DM)
        enc = sb("enc", P, TT * DM)
        xb = sb("xb", P, TT * DM)
        h = sb("h", P, TT * DM)
        hT = sb("hT", P, CG, SEQ)
        encT = sb("encT", P, CG, SEQ)
        qT = sb("qT", P, 2, CG, SEQ)
        kT = sb("kT", P, 2, CG, SEQ)
        k_head = sb("k_head", P, 2, HPG, SEQ)
        v = sb("v", P, 2, TT * DM)
        ctxT = sb("ctxT", P, CG, SEQ)
        score = sb("score", P, 2, TT * SEQ)
        prob = sb("prob", P, 4, TT * SEQ)
        probT = sb("probT", P, 2, 2 * SEQ)
        f1T = sb("f1T", P, 2, CG, SEQ)
        low = sb("low", P, NH, TT)
        rowsum = sb("rowsum", P, NH, TT)
        rowinv = sb("rowinv", P, NH, TT)
        stats = sb("stats", P, TT, 6)
        meanvar = sb("meanvar", P, TT, 2)
        std = sb("std", P, TT)
        rstd = sb("rstd", P, TT)
        eps_col = sb("eps_col", P, 1)

        G = [psum("G0"), psum("G1")]
        S = [psum("S0"), psum("S1")]
        PT = [psum("PT0"), psum("PT1")]
        O = [psum("O0"), psum("O1")]

        G_TILES = [("main", "xk", "act")] * 2 + [("main", "xv", "dve")] + [("main", "ao", "dve")] * 2 \
            + [("main", "xv", "dve")] + [("main", "hT2", "act")] * 2 + [("main", "xq", "dve")] * 2 \
            + [("next", "encT", "act")] * 2 + [("next", "hT1", "act")] * 2 + [("next", "q", "dve")] * 2 \
            + [("next", "k", "act")] * 2 + [("next", "v", "dve")] + [("main", "co", "dve")] * 2 \
            + [("next", "v", "dve")] + [("main", "hT3", "act")] * 2 + [("main", "f1", "act")] * (2 * FQ)
        assert len(G_TILES) % 2 == 0
        place = {}
        for n, (_, name, _) in enumerate(G_TILES):
            place.setdefault(name, []).append(n)

        def tiles_upto(n, stream, who=None):
            return sum(t[0] == stream and who in (None, t[2]) for t in G_TILES[:n + 1])

        ALL = len(G_TILES) - 1
        FF_STEPS = [(1, 0)] + [step for q in range(FQ - 1) for step in ((1, q + 1), (2, q))] + [(2, FQ - 1)]
        vectors_in = sem("vectors_in")
        self_mask_in = sem("self_mask_in")
        w_qkv_in = sem("w_qkv_in")
        weights_in = sem("weights_in")
        consts_made = sem("consts_made")
        self_filled = sem("self_filled")
        x_in = Tally(sem("x_in"), 1, 16)
        enc_in = Tally(sem("enc_in"), 1, 16)
        mask_in = Tally(sem("mask_in"), 1, 16)
        ring_in = [Tally(sem(f"ring_in{i}"), FQ, 16) for i in range(2)]
        w2_used = Tally(sem("w2_used"), FQ - 1, by="pe")
        g_full = {st: Tally(sem("g_full_" + st), tiles_upto(ALL, st), by="pe") for st in ("main", "next")}
        g_taken = {(st, e): Tally(sem(f"g_taken_{st}_{e}"), tiles_upto(ALL, st, e), by=e)
                   for st in ("main", "next") for e in ("act", "dve")}
        s_full = Tally(sem("s_full"), 2 * NH, by="pe")
        s_taken = Tally(sem("s_taken"), 2 * NH, by="dve")
        pt_full = Tally(sem("pt_full"), 2 * NH)
        pt_taken = Tally(sem("pt_taken"), 2 * NH, by="act")
        o_full = Tally(sem("o_full"), 2 * CG + TT, by="pe")
        o_taken = Tally(sem("o_taken"), 2 * CG + TT, by="dve")
        low_made = Tally(sem("low_made"), 2 * NH, by="dve")
        exp_done = Tally(sem("exp_done"), 2 * NH)
        inv_made = Tally(sem("inv_made"), 2 * NH)
        prob_made = Tally(sem("prob_made"), 2 * NH)
        khead_made = Tally(sem("khead_made"), 2 * NH)
        norms = {"next": 1, "main": 2}
        var_made = {st: Tally(sem("var_made_" + st), n) for st, n in norms.items()}
        std_made = {st: Tally(sem("std_made_" + st), n) for st, n in norms.items()}
        h_made = {st: Tally(sem("h_made_" + st), n) for st, n in norms.items()}
        xb_made = Tally(sem("xb_made"), 3, by="pool")
        x_out = Tally(sem("x_out"), 1, 16, by="act")
        links = {st: Tally(sem("links_" + st), n * (TT + 1)) for st, n in norms.items()}
        fill_made = Tally(sem("fill_made"), 1)

        def alone(eng):
            eng.nop(nofuse=True)

        def g_bank(name, k):
            return G[place[name][k] % 2]

        def g_filled(b, name, k):
            n = place[name][k]
            st = G_TILES[n][0]
            return g_full[st].sem, g_full[st].at(b, tiles_upto(n, st))

        def g_emptied(b, name, k):
            n = place[name][k]
            st, _, who = G_TILES[n]
            return g_taken[st, who].sem, g_taken[st, who].at(b, tiles_upto(n, st, who))

        def g_free(b, streams, name, k):
            n = place[name][k] - 2
            while n >= 0 and G_TILES[n][0] not in streams:
                n -= 2
            if n < 0:
                return [] if "main" not in streams else [
                    (g_taken["main", "act"].sem, g_taken["main", "act"].at(b, 0)),
                    (g_taken["next", "dve"].sem, g_taken["next", "dve"].at(b, g_taken["next", "dve"].per))]
            st, _, who = G_TILES[n]
            return [(g_taken[st, who].sem, g_taken[st, who].at(b + (st == "next"), tiles_upto(n, st, who)))]

        vi = {name: i for i, name in enumerate(T["vecs_a"])}
        block = ctx.enter_context(nc.Block())

        N_VECTOR_DMAS = len(T["vecs_a"]) + 1
        N_WEIGHT_DMAS = 4 + 3

        @block.sync
        def _(sp):
            def load_x(b):
                sp.dma_start(x_new[:, :].rearrange("p (a n) -> p a n", a=TT),
                             T["x"][b, :, :].rearrange("(a p) n -> p a n", p=P)).then_inc(x_in.sem, 16)

            def load_enc(b):
                sp.dma_start(enc[:, :].rearrange("p (a n) -> p a n", a=TT),
                             T["enc"][b, :, :].rearrange("(a p) n -> p a n", p=P)).then_inc(enc_in.sem, 16)

            def iteration(b, more):
                sp.wait_ge(low_made.sem, low_made.at(b, 0))
                alone(sp)
                sp.dma_start(mask[:, 1, :].rearrange("p (a k) -> p a k", a=TT),
                             T["mask_cross"][b, :, :].rearrange("(a p) k -> p a k", p=P)).then_inc(mask_in.sem, 16)
                for n, (layer, quarter) in enumerate(FF_STEPS):
                    if n == 0:
                        sp.wait_ge(w2_used.sem, w2_used.at(b, 0))
                    elif n == 1:
                        sp.wait_ge(o_full.sem, o_full.at(b, 0))
                    elif FF_STEPS[n - 2][0] == 1:
                        sp.wait_ge(*g_filled(b, "f1", 2 * FF_STEPS[n - 2][1] + 1))
                    else:
                        sp.wait_ge(w2_used.sem, w2_used.at(b, FF_STEPS[n - 2][1] + 1))
                    alone(sp)
                    if layer == 1:
                        part = T["w1"].rearrange("(c p) n -> p c n", p=P)[:, :, quarter * DM:(quarter + 1) * DM]
                    else:
                        part = T["w2"][quarter * DM:(quarter + 1) * DM, :].rearrange("(c p) n -> p c n", p=P)
                    sp.dma_start(ring[:, n % 2, :].rearrange("p (c n) -> p c n", c=CG), part)\
                        .then_inc(ring_in[n % 2].sem, 16)
                    if n == 1 and more:
                        sp.wait_ge(xb_made.sem, xb_made.at(b, 1))
                        alone(sp)
                        load_x(b + 1)
                        sp.wait_ge(*g_filled(b, "encT", 1))
                        alone(sp)
                        load_enc(b + 1)

            load_x(0)
            load_enc(0)
            with nc.allow_non_contiguous_dma(reason="channel vectors, once"):
                for name, i in vi.items():
                    sp.dma_start(vec[:, i, :], T[name].rearrange("(c p) -> p c", p=P)).then_inc(vectors_in, 16)
                sp.dma_start(b1_col[:, :], T["b1"].rearrange("(c p) -> p c", p=P)).then_inc(vectors_in, 16)
            sp.dma_start(w_qkv[:, :, :], T["w_qkv"].rearrange("(c p) n -> p c n", p=P)).then_inc(w_qkv_in, 16)
            sp.dma_start(mask[:, 0, :].rearrange("p (a k) -> p a k", a=TT),
                         T["mask_self"].rearrange("(a p) k -> p a k", p=P)).then_inc(self_mask_in, 16)
            for name, tile in (("w_kv", w_kv), ("w_ao", w_ao), ("w_q", w_q), ("w_co", w_co)):
                sp.dma_start(tile[:, :, :], T[name].rearrange("(c p) n -> p c n", p=P)).then_inc(weights_in, 16)
            for i, name in enumerate(("b_ao", "b_co", "b2")):
                sp.dma_start(bias_all[:, i, :], T[name].rearrange("(a n) -> a n", a=1).to_broadcast([P, DM]))\
                    .then_inc(weights_in, 16)
            with sp.Fori(0, BATCH - 1) as b:
                iteration(b, True)
            iteration(BATCH - 1, False)

        @block.gpsimd
        def _(pool):
            nc.gpsimd.memset(ident[:, :], 0.0).then_inc(consts_made, 1)
            nc.gpsimd.memset(eps_col[:, :], EPS)
            nc.gpsimd.memset(head_row[:, :], 1.0).then_inc(consts_made, 1)
            pool.wait_ge(consts_made, 2)
            nc.gpsimd.affine_select(out=ident[:, :], in_=ident[:, :], compare_op=ALU.not_equal, fill=1.0, base=0,
                                    pattern=[[-1, P]], channel_multiplier=1).then_inc(consts_made, 1)
            nc.gpsimd.affine_select(out=head_row[:, :], in_=head_row[:, :], compare_op=ALU.is_ge, fill=0.0, base=0,
                                    pattern=[[-HD, HPG]], channel_multiplier=1).then_inc(consts_made, 1)
            pool.wait_ge(consts_made, 4)
            nc.gpsimd.affine_select(out=head_row[:, :], in_=head_row[:, :], compare_op=ALU.is_ge, fill=0.0,
                                    base=HD - 1, pattern=[[HD, HPG]], channel_multiplier=-1).then_inc(consts_made, 1)
            pool.wait_ge(consts_made, 5)
            pool.wait_ge(weights_in, 16 * N_WEIGHT_DMAS)

            def add_bias(b, i, src):
                nc.gpsimd.tensor_tensor(xb[:, :].rearrange("p (a n) -> p a n", a=TT),
                                        src.rearrange("p (a n) -> p a n", a=TT),
                                        bias_all[:, i:i + 1, :].to_broadcast([P, TT, DM]), ALU.add)\
                    .then_inc(xb_made.sem, 1)

            def khead(b, at, hh):
                g, j = hh // HPG, hh % HPG
                if j == 0:
                    pool.wait_ge(s_full.sem, s_full.at(b, max(at * NH + (g - 1) * HPG, 0)))
                    alone(pool)
                if hh % (2 * HPG) == 0:
                    pool.wait_ge(*g_emptied(b, "xk" if at else "k", g // 2))
                    alone(pool)
                nc.gpsimd.tensor_scalar(k_head[:, g % 2, j, :], kT[:, at, g, :], head_row[:, j:j + 1], None, ALU.mult)\
                    .then_inc(khead_made.sem, 1)

            xb_made.prime(pool)
            with pool.Fori(0, BATCH) as b:
                for hh in range(2 * HPG):
                    khead(b, 0, hh)
                pool.wait_ge(x_in.sem, x_in.at(b, 1))
                alone(pool)
                pool.wait_ge(o_taken.sem, o_taken.at(b, 0))
                add_bias(b, 0, x_new[:, :])
                for hh in range(2 * HPG, NH):
                    khead(b, 0, hh)
                for hh in range(2 * HPG):
                    khead(b, 1, hh)
                pool.wait_ge(*g_emptied(b, "ao", 1))
                add_bias(b, 1, x[:, :])
                for hh in range(2 * HPG, NH):
                    khead(b, 1, hh)
                pool.wait_ge(*g_emptied(b, "co", 1))
                add_bias(b, 2, x[:, :])

        @block.tensor
        def _(pe):
            pe.wait_ge(consts_made, 5)

            def claim(b, streams, name, k):
                for tally, value in g_free(b, streams, name, k):
                    pe.wait_ge(tally, value)
                return g_bank(name, k), g_full[G_TILES[place[name][k]][0]].sem

            def turn(b, streams, name, k, src):
                bank, full = claim(b, streams, name, k)
                for c in range(2):
                    for a in range(TT):
                        col = (2 * k + c) * P
                        last = nc.tensor.transpose(bank[:, c * SEQ + a * P:c * SEQ + (a + 1) * P],
                                                   src[:, a * DM + col:a * DM + col + P], ident[:, :])
                last.then_inc(full, 1)

            def project_T(b, streams, name, k, w, col, actT, parts=range(PARTS)):
                for part in parts:
                    if part == 0:
                        claim(b, streams, name, k)
                    m = part // 2
                    for c in range(CG // 2 * (part % 2), CG // 2 * (part % 2 + 1)):
                        last = nc.tensor.matmul(g_bank(name, k)[:, m * SEQ:(m + 1) * SEQ],
                                                w[:, c, col + m * P:col + (m + 1) * P], actT[:, c, :],
                                                start=(c == 0), stop=(c == CG - 1))
                    if part == PARTS - 1:
                        last.then_inc(g_full[G_TILES[place[name][k]][0]].sem, 1)

            def project(b, streams, name, a, w, col, actT, parts=range(PARTS)):
                for c in parts:
                    if c == 0:
                        claim(b, streams, name, a)
                    last = nc.tensor.matmul(g_bank(name, a)[:, :], actT[:, c, a * P:(a + 1) * P],
                                            w[:, c, col:col + DM], start=(c == 0), stop=(c == CG - 1))
                    if c == PARTS - 1:
                        last.then_inc(g_full[G_TILES[place[name][a]][0]].sem, 1)

            def attend(b, at, between):
                def scores(hh):
                    n = at * NH + hh
                    g, j = hh // HPG, hh % HPG
                    if hh == 0 or hh == 2 * HPG:
                        pe.wait_ge(*g_emptied(b, "xq" if at else "q", g // 2))
                    pe.wait_ge(khead_made.sem, khead_made.at(b, n + 1))
                    pe.wait_ge(s_taken.sem, s_taken.at(b, max(n - 1, 0)))
                    for a in range(TT):
                        last = nc.tensor.matmul(S[n % 2][:, a * SEQ:(a + 1) * SEQ], qT[:, at, g, a * P:(a + 1) * P],
                                                k_head[:, g % 2, j, :], start=True, stop=True)
                    last.then_inc(s_full.sem, 1)

                def turn_probs(hh):
                    n = at * NH + hh
                    pe.wait_ge(prob_made.sem, prob_made.at(b, n + 1))
                    pe.wait_ge(pt_taken.sem, pt_taken.at(b, max(n - 1, 0)))
                    for k in range(2):
                        for a in range(TT):
                            last = nc.tensor.transpose(PT[n % 2][:, k * SEQ + a * P:k * SEQ + (a + 1) * P],
                                                       prob[:, hh % 4, a * SEQ + k * P:a * SEQ + (k + 1) * P],
                                                       ident[:, :])
                    last.then_inc(pt_full.sem, 1)

                def contexts(hh):
                    n = at * NH + hh
                    g, j = hh // HPG, hh % HPG
                    pe.wait_ge(pt_taken.sem, pt_taken.at(b, n + 1))
                    if j == 0:
                        pe.wait_ge(o_taken.sem, o_taken.at(b, max(at * CG + g - 1, 0)))
                    if hh == 0:
                        pe.wait_ge(*g_emptied(b, "xv" if at else "v", 1))
                    for k in range(2):
                        last = nc.tensor.matmul(O[g % 2][j * HD:(j + 1) * HD, 0:SEQ],
                                                v[:, at, k * DM + hh * HD:k * DM + (hh + 1) * HD],
                                                probT[:, n % 2, k * SEQ:(k + 1) * SEQ],
                                                start=(k == 0), stop=(k == 1))
                    if j == HPG - 1:
                        last.then_inc(o_full.sem, 1)

                for i in range(NH + 5):
                    if i < NH:
                        scores(i)
                    if 4 <= i < NH + 4:
                        turn_probs(i - 4)
                    if i >= 5:
                        contexts(i - 5)
                    for part in between.get(i, []):
                        part()

            def encoder(b, streams, k):
                if k == 0:
                    pe.wait_ge(enc_in.sem, enc_in.at(b + 1, 1))
                turn(b, streams, "encT", k, enc)

            def hidden_in(b, streams, k):
                if k == 0:
                    pe.wait_ge(h_made["next"].sem, h_made["next"].at(b + 1, 1))
                turn(b, streams, "hT1", k, h)

            def self_q(b, streams, k, parts=range(PARTS)):
                if 0 in parts:
                    pe.wait_ge(*g_emptied(b + 1, "hT1", 1))
                project_T(b, streams, "q", k, w_qkv, k * 2 * P, hT, parts)

            def self_k(b, streams, k, parts=range(PARTS)):
                project_T(b, streams, "k", k, w_qkv, DM + k * 2 * P, hT, parts)

            def self_v(b, streams, k, parts=range(PARTS)):
                project(b, streams, "v", k, w_qkv, 2 * DM, hT, parts)

            def iteration(b, streams):
                more = "next" in streams
                pe.wait_ge(*g_emptied(b, "encT", 1))
                work = [lambda p=p, k=k: project_T(b, streams, "xk", k, w_kv, k * 2 * P, encT, (p,))
                        for k in range(2) for p in range(PARTS)]
                work += [lambda p=p: project(b, streams, "xv", 0, w_kv, DM, encT, (p,)) for p in range(PARTS)]
                attend(b, 0, {3 + i: [part] for i, part in enumerate(work)})
                pe.wait_ge(o_taken.sem, o_taken.at(b, CG))
                for k in range(TT):
                    project(b, streams, "ao", k, w_ao, 0, ctxT)
                project(b, streams, "xv", 1, w_kv, DM, encT)
                pe.wait_ge(h_made["main"].sem, h_made["main"].at(b, 1))
                for k in range(2):
                    turn(b, streams, "hT2", k, h)
                pe.wait_ge(*g_emptied(b, "hT2", 1))
                for k in range(2):
                    project_T(b, streams, "xq", k, w_q, k * 2 * P, hT)
                between = {}
                if more:
                    turns = [lambda k=k, f=f: f(b, streams, k) for f in (encoder, hidden_in) for k in range(2)]
                    work = [lambda p=p, k=k, f=f: f(b, streams, k, (p,)) for f, k in (
                        (self_q, 0), (self_q, 1), (self_k, 0), (self_k, 1), (self_v, 0)) for p in range(PARTS)]
                    steps = [1, 2, 4, 5] + list(range(7, 15)) + [i for i in range(15, 21) for _ in range(2)]
                    for i, part in zip(steps, turns + work):
                        between.setdefault(i, []).append(part)
                attend(b, 1, between)
                pe.wait_ge(o_taken.sem, o_taken.at(b, 2 * CG))
                for k in range(TT):
                    project(b, streams, "co", k, w_co, 0, ctxT)
                if more:
                    self_v(b, streams, 1)
                pe.wait_ge(h_made["main"].sem, h_made["main"].at(b, 2))
                for k in range(2):
                    turn(b, streams, "hT3", k, h)
                pe.wait_ge(*g_emptied(b, "hT3", 1))

                def hidden(quarter, n):
                    pe.wait_ge(ring_in[n % 2].sem, ring_in[n % 2].at(b, n // 2 + 1))
                    for k in range(2):
                        project_T(b, streams, "f1", 2 * quarter + k, ring[:, n % 2, :].rearrange("p (c n) -> p c n", c=CG),
                                  k * 2 * P, hT)

                def output(quarter, n):
                    pe.wait_ge(ring_in[n % 2].sem, ring_in[n % 2].at(b, n // 2 + 1))
                    pe.wait_ge(*g_emptied(b, "f1", 2 * quarter + 1))
                    w2 = ring[:, n % 2, :].rearrange("p (c n) -> p c n", c=CG)
                    for a in range(TT):
                        for c in range(CG):
                            last = nc.tensor.matmul(O[a][:, :], f1T[:, quarter % 2, c, a * P:(a + 1) * P], w2[:, c, :],
                                                    start=(quarter == 0 and c == 0),
                                                    stop=(quarter == FQ - 1 and c == CG - 1))
                        if quarter == FQ - 1:
                            last.then_inc(o_full.sem, 1)
                    if quarter < FQ - 1:
                        last.then_inc(w2_used.sem, 1)

                for n, (layer, quarter) in enumerate(FF_STEPS):
                    (hidden if layer == 1 else output)(quarter, n)

            for tally in (g_full["main"], g_full["next"], o_full, s_full, w2_used):
                tally.prime(pe)
            for step in (encoder, hidden_in, self_q, self_k, self_v):
                if step is self_q:
                    pe.wait_ge(w_qkv_in, 16)
                for k in range(2):
                    step(-1, ("next",), k)
            pe.wait_ge(weights_in, 16 * N_WEIGHT_DMAS)
            with pe.Fori(0, BATCH - 1) as b:
                iteration(b, ("main", "next"))
            iteration(BATCH - 1, ("main",))

        @block.vector
        def _(dve):
            def layernorm(b, st, i, src, meanwhile=None):
                at = i * (TT + 1)
                for a in range(TT):
                    nc.vector.bn_stats(stats[:, a, :], src[:, a * DM:(a + 1) * DM]).then_inc(links[st].sem, 1)
                dve.wait_ge(links[st].sem, links[st].at(b, at + TT))
                alone(dve)
                for a in range(TT):
                    last = nc.vector.bn_aggr(meanvar[:, a, :], stats[:, a, :])
                last.then_inc(var_made[st].sem, 1)
                if meanwhile:
                    meanwhile()
                dve.wait_ge(std_made[st].sem, std_made[st].at(b, i + 1))
                nc.vector.reciprocal(rstd[:, :], std[:, :]).then_inc(links[st].sem, 1)
                dve.wait_ge(links[st].sem, links[st].at(b, at + TT + 1))
                for a in range(TT):
                    last = nc.vector.tensor_scalar(h[:, a * DM:(a + 1) * DM], src[:, a * DM:(a + 1) * DM],
                                                   meanvar[:, a, 0:1], rstd[:, a:a + 1], ALU.subtract, ALU.mult)
                last.then_inc(h_made[st].sem, 1)

            def take_q(b, name, at, bias, k):
                dve.wait_ge(*g_filled(b, name, k))
                for m in range(2):
                    last = nc.vector.tensor_scalar(qT[:, at, 2 * k + m, :], g_bank(name, k)[:, m * SEQ:(m + 1) * SEQ],
                                                   vec[:, vi[bias], 2 * k + m:2 * k + m + 1], None, ALU.add)
                last.then_inc(g_taken["main" if at else "next", "dve"].sem, 1)

            def take_v(b, name, at, k):
                dve.wait_ge(*g_filled(b, name, k))
                nc.vector.tensor_copy(v[:, at, k * DM:(k + 1) * DM], g_bank(name, k)[:, :])\
                    .then_inc(g_taken["main" if at else "next", "dve"].sem, 1)

            def take_x(b, name):
                for k in range(TT):
                    dve.wait_ge(*g_filled(b, name, k))
                    nc.vector.tensor_tensor(x[:, k * DM:(k + 1) * DM], g_bank(name, k)[:, :],
                                            xb[:, k * DM:(k + 1) * DM], ALU.add)\
                        .then_inc(g_taken["main", "dve"].sem, 1)
                dve.wait_ge(*g_emptied(b, name, TT - 1))

            def attend(b, at, bias, between):
                def invert(hh):
                    n = at * NH + hh
                    dve.wait_ge(exp_done.sem, exp_done.at(b, n + 1))
                    return nc.vector.reciprocal(rowinv[:, hh, :], rowsum[:, hh, :])

                def take_context(g):
                    dve.wait_ge(o_full.sem, o_full.at(b, at * CG + g + 1))
                    nc.vector.tensor_scalar(ctxT[:, g, :], O[g % 2][:, 0:SEQ], vec[:, vi[bias], g:g + 1], None,
                                            ALU.add).then_inc(o_taken.sem, 1)

                def normalize(hh):
                    n = at * NH + hh
                    dve.wait_ge(inv_made.sem, inv_made.at(b, n + 1))
                    for a in range(TT):
                        q = prob[:, hh % 4, a * SEQ:(a + 1) * SEQ]
                        last = nc.vector.tensor_scalar(q, q, rowinv[:, hh, a:a + 1], None, ALU.mult)
                    last.then_inc(prob_made.sem, 1)

                for i in range(NH):
                    n = at * NH + i
                    dve.wait_ge(s_full.sem, s_full.at(b, n + 1))
                    if n >= 2:
                        dve.wait_ge(exp_done.sem, exp_done.at(b, n - 1))
                    nc.vector.scalar_tensor_tensor(out=score[:, i % 2, :], in0=S[n % 2][:, :], scalar=-SCORE_SCALE,
                                                   in1=mask[:, at, :], op0=ALU.mult, op1=ALU.mult)\
                        .then_inc(s_taken.sem, 1)
                    dve.wait_ge(s_taken.sem, s_taken.at(b, n + 1))
                    if i < 2:
                        alone(dve)
                    else:
                        invert(i - 2).then_inc(inv_made.sem, 1)
                    for a in range(TT):
                        sc = score[:, i % 2, a * SEQ:(a + 1) * SEQ]
                        last = nc.vector.tensor_tensor_reduce(sc, sc, fill[:, at, a * SEQ:(a + 1) * SEQ], 1.0, 3.0e38,
                                                              ALU.add, ALU.min, low[:, i, a:a + 1])
                    last.then_inc(low_made.sem, 1)
                    if i >= 2:
                        normalize(i - 2)
                    if i >= 9 and (i - 9) % HPG == 0:
                        take_context((i - 9) // HPG)
                    if i in between:
                        between[i]()
                for i in (NH - 2, NH - 1):
                    invert(i).then_inc(inv_made.sem, 1)
                    normalize(i)
                for g in range(2, CG):
                    take_context(g)

            def iteration(b, more):
                attend(b, 0, "b_v1", {15: lambda: take_v(b, "xv", 1, 0)})
                dve.wait_ge(xb_made.sem, xb_made.at(b, 1))
                dve.wait_ge(x_out.sem, x_out.at(b, 0))
                take_x(b, "ao")
                layernorm(b, "main", 0, x, lambda: take_v(b, "xv", 1, 1))
                for k in range(2):
                    take_q(b, "xq", 1, "b_q", k)
                dve.wait_ge(mask_in.sem, mask_in.at(b, 1))
                nc.vector.tensor_scalar(fill[:, 1, :], mask[:, 1, :], -MASKED, MASKED, ALU.mult, ALU.add)\
                    .then_inc(fill_made.sem, 1)
                dve.wait_ge(fill_made.sem, fill_made.at(b, 1))

                def norm_next():
                    dve.wait_ge(x_in.sem, x_in.at(b + 1, 1))
                    layernorm(b + 1, "next", 0, x_new)

                attend(b, 1, "b_v2", {
                    2: norm_next,
                    11: lambda: take_q(b + 1, "q", 0, "b_q1", 0),
                    15: lambda: take_q(b + 1, "q", 0, "b_q1", 1),
                } if more else {})
                if more:
                    take_v(b + 1, "v", 0, 0)
                dve.wait_ge(xb_made.sem, xb_made.at(b, 2))
                take_x(b, "co")
                layernorm(b, "main", 1, x, (lambda: take_v(b + 1, "v", 0, 1)) if more else None)
                dve.wait_ge(xb_made.sem, xb_made.at(b, 3))
                for a in range(TT):
                    dve.wait_ge(o_full.sem, o_full.at(b, 2 * CG + a + 1))
                    nc.vector.tensor_tensor(x[:, a * DM:(a + 1) * DM], O[a][:, :], xb[:, a * DM:(a + 1) * DM],
                                            ALU.add).then_inc(o_taken.sem, 1)

            for tally in (g_taken["main", "dve"], g_taken["next", "dve"], low_made, o_taken, s_taken):
                tally.prime(dve)
            dve.wait_ge(x_in.sem, x_in.at(0, 1))
            layernorm(0, "next", 0, x_new)
            dve.wait_ge(self_mask_in, 16)
            nc.vector.tensor_scalar(fill[:, 0, :], mask[:, 0, :], -MASKED, MASKED, ALU.mult, ALU.add)\
                .then_inc(self_filled, 1)
            dve.wait_ge(self_filled, 1)
            dve.wait_ge(vectors_in, 16 * N_VECTOR_DMAS)
            for k in range(2):
                take_q(0, "q", 0, "b_q1", k)
            for k in range(TT):
                take_v(0, "v", 0, k)
            with dve.Fori(0, BATCH - 1) as b:
                iteration(b, True)
            iteration(BATCH - 1, False)

        @block.scalar
        def _(act):
            act.wait_ge(vectors_in, 16 * N_VECTOR_DMAS)
            act.wait_ge(consts_made, 5)

            def root(b, st, i):
                act.wait_ge(var_made[st].sem, var_made[st].at(b, i + 1))
                nc.scalar.activation(std[:, :], meanvar[:, :, 1], ACT.Sqrt, bias=eps_col[:, :])\
                    .then_inc(std_made[st].sem, 1)

            def take_T(b, name, k, dst, scale, bias):
                act.wait_ge(*g_filled(b, name, k))
                bank = g_bank(name, k)
                if scale is None and bias is None:
                    last = nc.scalar.activation(dst[:, 2 * k:2 * k + 2, :].rearrange("p c t -> p (c t)"),
                                                bank[:, :], ACT.Copy)
                else:
                    for m in range(2):
                        c = 2 * k + m
                        last = nc.scalar.activation(dst[:, c, :], bank[:, m * SEQ:(m + 1) * SEQ], ACT.Identity,
                                                    bias=vec[:, vi[bias], c:c + 1],
                                                    scale=1.0 if scale is None else vec[:, vi[scale], c:c + 1])
                last.then_inc(g_taken[G_TILES[place[name][k]][0], "act"].sem, 1)

            def attend(b, at, between):
                def exponentials(hh):
                    n = at * NH + hh
                    act.wait_ge(low_made.sem, low_made.at(b, n + 1))
                    if n >= 4:
                        act.wait_ge(pt_full.sem, pt_full.at(b, n - 3))
                    for a in range(TT):
                        last = nc.scalar.activation(prob[:, hh % 4, a * SEQ:(a + 1) * SEQ],
                                                    score[:, hh % 2, a * SEQ:(a + 1) * SEQ], ACT.Exp,
                                                    bias=low[:, hh, a:a + 1], scale=-1.0,
                                                    accum_out=rowsum[:, hh, a:a + 1])
                    last.then_inc(exp_done.sem, 1)

                def take_probs(hh):
                    n = at * NH + hh
                    act.wait_ge(pt_full.sem, pt_full.at(b, n + 1))
                    nc.scalar.activation(probT[:, n % 2, :], PT[n % 2][:, :], ACT.Copy).then_inc(pt_taken.sem, 1)

                for i in range(NH + 4):
                    if i < NH:
                        exponentials(i)
                    if i >= 4:
                        take_probs(i - 4)
                    if i in between:
                        between[i]()

            def encoder(b, k):
                take_T(b, "encT", k, encT, None, None)

            def hidden_in(b, k):
                take_T(b, "hT1", k, hT, "ln1_s", "ln1_b")

            def self_k(b, k):
                take_T(b, "k", k, kT[:, 0, :, :], None, "b_k1")

            def iteration(b, more):
                attend(b, 0, {
                    7: lambda: take_T(b, "xk", 0, kT[:, 1, :, :], None, "b_k2"),
                    11: lambda: take_T(b, "xk", 1, kT[:, 1, :, :], None, "b_k2"),
                })
                root(b, "main", 0)
                for k in range(2):
                    take_T(b, "hT2", k, hT, "ln2_s", "ln2_b")
                attend(b, 1, {
                    2: lambda: root(b + 1, "next", 0),
                    3: lambda: encoder(b + 1, 0),
                    4: lambda: encoder(b + 1, 1),
                    5: lambda: hidden_in(b + 1, 0),
                    6: lambda: hidden_in(b + 1, 1),
                    17: lambda: self_k(b + 1, 0),
                    19: lambda: self_k(b + 1, 1),
                } if more else {})
                root(b, "main", 1)
                for k in range(2):
                    take_T(b, "hT3", k, hT, "ln3_s", "ln3_b")
                for i in range(2 * FQ):
                    quarter, k = i // 2, i % 2
                    act.wait_ge(*g_filled(b, "f1", i))
                    if k == 0 and quarter >= 2:
                        act.wait_ge(w2_used.sem, w2_used.at(b, quarter - 1))
                    for m in range(2):
                        last = nc.scalar.activation(f1T[:, quarter % 2, 2 * k + m, :],
                                                    g_bank("f1", i)[:, m * SEQ:(m + 1) * SEQ], ACT.Gelu_apprx_tanh,
                                                    bias=b1_col[:, 2 * i + m:2 * i + m + 1])
                    last.then_inc(g_taken["main", "act"].sem, 1)
                act.wait_ge(o_taken.sem, o_taken.at(b, 2 * CG + TT))
                alone(act)
                act.dma_start(x3_dram[b, :, :].rearrange("(a p) n -> p a n", p=P),
                              x[:, :].rearrange("p (a n) -> p a n", a=TT)).then_inc(x_out.sem, 16)

            for tally in (g_taken["main", "act"], g_taken["next", "act"], pt_taken, x_out):
                tally.prime(act)
            encoder(0, 0)
            encoder(0, 1)
            root(0, "next", 0)
            hidden_in(0, 0)
            hidden_in(0, 1)
            self_k(0, 0)
            self_k(0, 1)
            with act.Fori(0, BATCH - 1) as b:
                iteration(b, True)
            iteration(BATCH - 1, False)
            act.wait_ge(x_out.sem, x_out.at(BATCH - 1, 1))


def vectors(T):
    T["b_q1"], T["b_k1"], T["b_v1"] = (T["b_qkv"][i * DM:(i + 1) * DM] for i in range(3))
    T["b_k2"], T["b_v2"] = (T["b_kv"][i * DM:(i + 1) * DM] for i in range(2))
    T["vecs_a"] = ["b_q1", "b_k1", "b_v1", "b_q", "b_k2", "b_v2", "ln1_s", "ln1_b", "ln2_s", "ln2_b", "ln3_s", "ln3_b"]


N_HEADS, HS = 32, 16
MIX = 5
MIX_RANK = 32
DECAY_RANK = 64
IQ, JP = 4, 2
IROWS, JCOLS = HS // IQ, 2
STEPS = IQ * JP
JOWN = 4


def vectors_b(T):
    for f in range(MIX):
        T[f"stack{f}"] = T["maa_stack"][0, f, :]
    T["u_flat"] = T["u"].rearrange("h s a -> (h s a)")
    T["vecs_b"] = ["m_ln1_w", "m_ln1_b", "m_ln2_w", "m_ln2_b", "maa_x", "time_decay", "u_flat", "gn_w", "gn_b",
                   "ffn_maa_k", "ffn_maa_r"] + [f"stack{f}" for f in range(MIX)]


def recurrent_block(nc, sems, T, x3_dram, out_dram):
    with ExitStack() as ctx:
        def sb(name, *shape):
            return ctx.enter_context(nc.sbuf_tensor("b_" + name, list(shape), F32))

        def sem(name):
            return sems.enter_context(nc.semaphore("b_" + name))

        def dram(name, *shape):
            return nc.dram_tensor("b_" + name, list(shape), F32, kind="Internal").ap()

        w_dram = dram("w_all", BATCH, DM, SEQ + 1)
        k_dram, v_dram, r_dram, g_dram, bv_dram, o_dram = (
            dram(n, BATCH, DM, SEQ) for n in ("k_all", "v_all", "r_all", "g_all", "bv_all", "o_all"))

        W = {n: sb(n, P, CG, DM) for n in ("Wk", "Wv", "Wr", "Wg", "Wo", "Wfr", "Wfk", "Wfv")}
        maa_w1 = sb("maa_w1", P, CG, 2 * P)
        maa_w2 = sb("maa_w2", P, 2, DM)
        td_w1 = sb("td_w1", P, CG, P)
        td_w2 = sb("td_w2", P, DM)
        vec = sb("vec", P, len(T["vecs_b"]), CG)
        ident = sb("ident", P, P)
        same_head = sb("same_head", P, P)
        mean_head = sb("mean_head", P, P)
        f_row = sb("f_row", P, MIX - 1)
        eps_col = sb("eps_col", P, 1)
        state_rows = sb("state_rows", 2 * BATCH, DM)
        stateT = sb("stateT", P, CG, 2 * BATCH)
        xa = sb("xa", P, TT, DM)
        xaT = sb("xaT", P, CG, SEQ + 1)
        sx = sb("sx", P, CG, SEQ)
        mixed = sb("mixed", P, 2, CG, SEQ)
        z = sb("z", P, CG, SEQ)
        t1 = sb("t1", P, 2, SEQ)
        t1f = sb("t1f", P, 2, SEQ)
        tdt = sb("tdt", P, SEQ)
        kT, vT, rT, gT = (sb(n, P, CG, SEQ) for n in ("kT", "vT", "rT", "gT"))
        wT = sb("wT", P, CG, SEQ + 1)
        stats = sb("stats", P, 2, TT, 6)
        meanvar = sb("meanvar", P, 2, TT, 2)
        std = sb("std", P, 2, TT)
        rstd = sb("rstd", P, 2, TT)
        ws = sb("ws", P, 2, IROWS, SEQ + 1)
        ks = sb("ks", P, 2, IROWS, SEQ)
        rs = sb("rs", P, 2, IROWS, SEQ)
        vs = sb("vs", P, JOWN, SEQ)
        s0 = sb("s0", P, HS, JOWN)
        ring = sb("ring", P, 2, JCOLS, IROWS, SEQ + 1)
        part = sb("part", P, JCOLS, SEQ)
        osum = sb("osum", P, JOWN, SEQ)
        o = sb("o", P, CG, SEQ)
        bv = sb("bv", P, CG, SEQ)
        g = sb("g", P, CG, SEQ)
        xr = sb("xr", P, TT, DM)
        sq = sb("sq", P, CG, SEQ)
        xcT = sb("xcT", P, CG, SEQ + 1)
        sx2 = sb("sx2", P, CG, SEQ)

        def psum(name):
            return ctx.enter_context(nc.psum_tensor("b_" + name, [P, 512], F32))

        BANKS = {st: [psum(f"{st}_bank{i}") for i in range(n)] for st, n in (("n", 2), ("a", 3), ("c", 3))}
        TILES = {
            "n": [("xaT", "act")] * 2 + [("t1", "act"), None],
            "a": [("mix0", "dve")] * 2 + [("mix1", "dve")] * 2
            + [("k", "act")] * 2 + [("mix2", "dve")] * 2 + [("td1", "act")] + [("mix3", "dve")] * 2
            + [("td2", "act")] * 2 + [("v", "act")] * 2 + [("mix4", "dve")] * 2 + [("r", "act")] * 2
            + [("g", "dve")] * 2 + [("bonus", "dve")] * 2 + [None],
            "c": [("mean", "dve")] * 2 + [("var", "act")] * 2 + [("wo", "dve")] * 2 + [("xcT", "act")] * 2
            + [("rr", "act")] * 2 + [("kk", "act")] * 2 + [("kv", "dve")] * 2 + [None],
        }
        first, full, taken = {}, {}, {}
        for part_name, tiles in TILES.items():
            assert len(tiles) % len(BANKS[part_name]) == 0
            for n, t in enumerate(tiles):
                if t:
                    first.setdefault(t[0], (part_name, n))
            full[part_name] = Tally(sem(f"{part_name}_full"), sum(t is not None for t in tiles), by="pe")
            taken[part_name] = {e: Tally(sem(f"{part_name}_taken_{e}"), sum(t is not None and t[1] == e for t in tiles),
                                         by=e)
                                for e in ("act", "dve") if any(t is not None and t[1] == e for t in tiles)}

        def tile(name, k):
            which, n = first[name]
            return BANKS[which][(n + k) % len(BANKS[which])]

        def upto(which, n, who):
            return sum(t is not None and who in (None, t[1]) for t in TILES[which][:n + 1])

        def filled(b, name, k):
            which, n = first[name]
            return full[which].sem, full[which].at(b, upto(which, n + k, None))

        def emptied(b, name, k):
            which, n = first[name]
            t = taken[which][TILES[which][n + k][1]]
            return t.sem, t.at(b, upto(which, n + k, TILES[which][n + k][1]))

        def bank_free(b, name, k):
            which, n = first[name]
            m = n + k - len(BANKS[which])
            while TILES[which][m] is None:
                m -= len(BANKS[which])
            t = taken[which][TILES[which][m][1]]
            return t.sem, t.at(b, upto(which, m, TILES[which][m][1]) if m >= 0 else 0)

        def full_sem(name):
            return full[first[name][0]].sem

        def empty_sem(name):
            which, n = first[name]
            return taken[which][TILES[which][n][1]].sem

        vectors_in = sem("vectors_in")
        weights_in = sem("weights_in")
        pads_made = sem("pads_made")
        consts_made = sem("consts_made")
        state_turned = sem("state_turned")
        state_kept = sem("state_kept")
        xa_in = Tally(sem("xa_in"), 1, 16)
        a_var = Tally(sem("a_var"), 1)
        a_std = Tally(sem("a_std"), 1)
        a_h = Tally(sem("a_h"), 1)
        sx_made = Tally(sem("sx_made"), 1)
        z_made = Tally(sem("z_made"), 1)
        f_made = Tally(sem("f_made"), MIX - 1)
        mix_made = Tally(sem("mix_made"), MIX)
        w_made = Tally(sem("w_made"), 1)
        kwvr_out = Tally(sem("kwvr_out"), 4, 16, by="act")
        tanh_g = Tally(sem("tanh_g"), 2)
        rku_made = Tally(sem("rku_made"), 2)
        g_out = Tally(sem("g_out"), 1, 16, by="sp")
        bv_out = Tally(sem("bv_out"), 1, 16, by="sp")
        wkr_in = [Tally(sem(f"wkr_in{i}"), IQ // 2, 48) for i in range(2)]
        vs_in = Tally(sem("vs_in"), 1, 80)
        kv_made = Tally(sem("kv_made"), STEPS, by="pool")
        scanned = Tally(sem("scanned"), STEPS)
        weighed = Tally(sem("weighed"), STEPS, by="dve")
        reduced = Tally(sem("reduced"), STEPS, by="dve")
        summed = Tally(sem("summed"), STEPS - JP)
        o_out = Tally(sem("o_out"), 1, 16, by="sp")
        o_in = Tally(sem("o_in"), 2, 16)
        c_in = Tally(sem("c_in"), 2, 16)
        o_made = Tally(sem("o_made"), 1)
        sq_made = Tally(sem("sq_made"), 1)
        rstd_made = Tally(sem("rstd_made"), 1)
        y_made = Tally(sem("y_made"), 1)
        yn_made = Tally(sem("yn_made"), 1)
        yg_made = Tally(sem("yg_made"), 1)
        c_var = Tally(sem("c_var"), 1)
        c_std = Tally(sem("c_std"), 1)
        c_h = Tally(sem("c_h"), 1)
        sx2_made = Tally(sem("sx2_made"), 1)
        xr_made = Tally(sem("xr_made"), 1)
        kk_made = Tally(sem("kk_made"), 1)
        rr_made = Tally(sem("rr_made"), 1)
        out_made = Tally(sem("out_made"), 1)
        out_out = Tally(sem("out_out"), 1, 16, by="sp")
        a_links = Tally(sem("a_links"), TT + 1)
        c_links = Tally(sem("c_links"), TT + 1)

        vi = {name: i for i, name in enumerate(T["vecs_b"])}

        def col(name, c):
            return vec[:, vi[name], c:c + 1]

        def alone(eng):
            eng.nop(nofuse=True)

        def pipeline(eng, body, after_first=None):
            body(0, None, None, None)
            if after_first:
                after_first()
            body(1, 0, None, None)
            body(2, 1, 0, None)
            with eng.Fori(0, BATCH - 3) as i:
                body(i + 3, i + 2, i + 1, i)
            body(None, BATCH - 1, BATCH - 2, BATCH - 3)
            body(None, None, BATCH - 1, BATCH - 2)
            body(None, None, None, BATCH - 1)

        def flat(ap):
            return ap.rearrange("p c t -> p (c t)")

        block = ctx.enter_context(nc.Block())
        N_FIRST_DMAS = len(vi) + 1 + 3
        N_WEIGHT_DMAS = 2 + len(W)

        @block.sync
        def _(sp):
            with nc.allow_non_contiguous_dma(reason="channel vectors, once"):
                for name, i in vi.items():
                    sp.dma_start(vec[:, i, :], T[name].rearrange("(c p) -> p c", p=P)).then_inc(vectors_in, 16)
            sp.dma_start(state_rows[:, :], T["enc"][:, 0:2, :]).then_inc(vectors_in, 16)
            sp.wait_ge(pads_made, 4)
            sp.dma_start(maa_w1[:, :, 0:MIX * MIX_RANK], T["maa_w1"].rearrange("(c p) n -> p c n", p=P))\
                .then_inc(vectors_in, 16)
            sp.dma_start(maa_w2[:, 0, :], T["maa_w2"][0:4, :, :].rearrange("f d n -> (f d) n")).then_inc(vectors_in, 16)
            sp.dma_start(maa_w2[0:MIX_RANK, 1, :], T["maa_w2"][4, :, :]).then_inc(vectors_in, 16)

            def load_weights():
                sp.dma_start(W["Wk"][:, :, :], T["Wk"].rearrange("(c p) n -> p c n", p=P)).then_inc(weights_in, 16)
                sp.dma_start(td_w1[:, :, 0:DECAY_RANK], T["td_w1"].rearrange("(c p) n -> p c n", p=P))\
                    .then_inc(weights_in, 16)
                sp.dma_start(td_w2[0:DECAY_RANK, :], T["td_w2"]).then_inc(weights_in, 16)
                for n in ("Wv", "Wr", "Wg", "Wo", "Wfr", "Wfk", "Wfv"):
                    sp.dma_start(W[n][:, :, :], T[n].rearrange("(c p) n -> p c n", p=P)).then_inc(weights_in, 16)

            def wkr(s, q):
                for tile_, dram_ in ((ws, w_dram), (ks, k_dram), (rs, r_dram)):
                    n = tile_.shape[-1]
                    rows = dram_[s, :, :].rearrange("(h q i) t -> h q (i t)", q=IQ, i=IROWS)[:, q:q + 1, :]
                    sp.dma_start(tile_[:, q % 2, :, :].rearrange("p i t -> p (i t)"),
                                 rows.to_broadcast([N_HEADS, P // N_HEADS, IROWS * n]))\
                        .then_inc(wkr_in[q % 2].sem, 16)

            def put(s, name, k, d, t, tally):
                sp.wait_ge(*emptied(s, name, k))
                alone(sp)
                sp.dma_start(d[s, :, :].rearrange("(c p) t -> p c t", p=P), t).then_inc(tally.sem, 16)

            def body(n, a, s, c):
                if n is not None:
                    if a is not None:
                        sp.wait_ge(*filled(a, "xaT", 1))
                        alone(sp)
                    sp.dma_start(xa[:, :, :], x3_dram[n, :, :].rearrange("(a p) n -> p a n", p=P))\
                        .then_inc(xa_in.sem, 16)
                if c is not None:
                    for tally in (bv_out, g_out):
                        sp.wait_ge(tally.sem, tally.at(c, 1))
                        alone(sp)
                    sp.dma_start(bv[:, :, :], bv_dram[c, :, :].rearrange("(c p) t -> p c t", p=P)).then_inc(o_in.sem, 16)
                    sp.dma_start(g[:, :, :], g_dram[c, :, :].rearrange("(c p) t -> p c t", p=P)).then_inc(c_in.sem, 16)
                    sp.wait_ge(o_out.sem, o_out.at(c, 1))
                    alone(sp)
                    sp.dma_start(o[:, :, :], o_dram[c, :, :].rearrange("(c p) t -> p c t", p=P)).then_inc(o_in.sem, 16)
                    sp.wait_ge(out_out.sem, out_out.at(c, 0))
                    alone(sp)
                    sp.dma_start(xr[:, :, :], x3_dram[c, :, :].rearrange("(a p) n -> p a n", p=P)).then_inc(c_in.sem, 16)
                if s is not None:
                    for q in range(2, IQ):
                        sp.wait_ge(weighed.sem, weighed.at(s, 2 * (q - 1)))
                        alone(sp)
                        wkr(s, q)
                if a is not None:
                    put(a, "g", 1, g_dram, gT[:, :, :], g_out)
                    sp.wait_ge(kwvr_out.sem, kwvr_out.at(a, 4))
                    alone(sp)
                    if s is not None:
                        sp.wait_ge(weighed.sem, weighed.at(s, STEPS - JP))
                        alone(sp)
                    wkr(a, 0)
                    sp.wait_ge(kv_made.sem, kv_made.at(a, 0))
                    alone(sp)
                    sp.dma_start(vs[:, :, :], v_dram[a, :, :].rearrange("(p j) t -> p j t", j=JOWN))\
                        .then_inc(vs_in.sem, 16)
                    starts = T["enc"][a, 2:2 + HS, :].rearrange("r (q i g j) -> (r q) g i j", q=DM // (HS * HS), i=HS,
                                                                j=JOWN)
                    for quad in range(P // N_HEADS):
                        sp.dma_start(s0[quad:P:P // N_HEADS, :, :], starts[:, quad, :, :]).then_inc(vs_in.sem, 16)
                    put(a, "bonus", 1, bv_dram, mixed[:, 0, :, :], bv_out)
                    sp.wait_ge(weighed.sem, weighed.at(a, 0))
                    alone(sp)
                    wkr(a, 1)
                if s is not None:
                    sp.wait_ge(summed.sem, summed.at(s, STEPS - JP))
                    alone(sp)
                    sp.dma_start(o_dram[s, :, :].rearrange("(p j) t -> p j t", j=JOWN), osum[:, :, :])\
                        .then_inc(o_out.sem, 16)
                if c is not None:
                    sp.wait_ge(out_made.sem, out_made.at(c, 1))
                    alone(sp)
                    sp.dma_start(out_dram[c, :, :].rearrange("(a p) n -> p a n", p=P), xr[:, :, :])\
                        .then_inc(out_out.sem, 16)

            for tally in (bv_out, g_out, o_out, out_out):
                tally.prime(sp)
            pipeline(sp, body, load_weights)
            sp.wait_ge(out_out.sem, out_out.at(BATCH - 1, 1))

        @block.gpsimd
        def _(pool):
            for t in (maa_w1[:, :, :], maa_w2[:, :, :], td_w1[:, :, :], td_w2[:, :]):
                nc.gpsimd.memset(t, 0.0).then_inc(pads_made, 1)
            nc.gpsimd.memset(ident[:, :], 0.0)
            nc.gpsimd.memset(eps_col[:, :], EPS)
            nc.gpsimd.memset(wT[:, :, 0:1], 0.0)
            nc.gpsimd.memset(same_head[:, :], 1.0)
            nc.gpsimd.memset(mean_head[:, :], 1.0 / HS)
            nc.gpsimd.memset(f_row[:, :], 1.0).then_inc(consts_made, 1)
            pool.wait_ge(consts_made, 1)
            nc.gpsimd.affine_select(out=ident[:, :], in_=ident[:, :], compare_op=ALU.not_equal, fill=1.0, base=0,
                                    pattern=[[-1, P]], channel_multiplier=1)
            blocks = ((same_head, HS, P // HS, HS), (mean_head, HS, P // HS, HS), (f_row, MIX_RANK, MIX - 1, 1))
            for t, size, n, width in blocks:
                v_ = t[:, :].rearrange("p (n w) -> p n w", w=width)
                last = nc.gpsimd.affine_select(out=v_, in_=v_, compare_op=ALU.is_ge, fill=0.0, base=0,
                                               pattern=[[-size, n], [0, width]], channel_multiplier=1)
            last.then_inc(consts_made, 1)
            pool.wait_ge(consts_made, 2)
            for t, size, n, width in blocks:
                v_ = t[:, :].rearrange("p (n w) -> p n w", w=width)
                last = nc.gpsimd.affine_select(out=v_, in_=v_, compare_op=ALU.is_ge, fill=0.0, base=size - 1,
                                               pattern=[[size, n], [0, width]], channel_multiplier=-1)
            last.then_inc(consts_made, 1)

            def outer(s, u):
                q, jp = u // JP, u % JP
                if u == 0:
                    pool.wait_ge(vs_in.sem, vs_in.at(s, 1))
                    alone(pool)
                if jp == 0:
                    pool.wait_ge(wkr_in[q % 2].sem, wkr_in[q % 2].at(s, q // 2 + 1))
                    alone(pool)
                pool.wait_ge(reduced.sem, reduced.at(s, max(u - 1, 0)))
                alone(pool)
                slot = ring[:, u % 2, :, :, :]
                for j in range(JCOLS):
                    nc.gpsimd.tensor_copy(slot[:, j, :, 0:1],
                                          s0[:, q * IROWS:(q + 1) * IROWS, jp * JCOLS + j:jp * JCOLS + j + 1])
                nc.gpsimd.tensor_tensor(slot[:, :, :, 1:SEQ + 1],
                                        ks[:, q % 2, :, :].unsqueeze(1).to_broadcast([P, JCOLS, IROWS, SEQ]),
                                        vs[:, jp * JCOLS:(jp + 1) * JCOLS, :].unsqueeze(2)
                                        .to_broadcast([P, JCOLS, IROWS, SEQ]), ALU.mult).then_inc(kv_made.sem, 1)

            def add_xa(a, f):
                pool.wait_ge(*emptied(a, f"mix{f}", 1))
                alone(pool)
                nc.gpsimd.tensor_tensor(mixed[:, f % 2, :, :], mixed[:, f % 2, :, :], xaT[:, :, 1:SEQ + 1], ALU.add)\
                    .then_inc(mix_made.sem, 1)

            def body(n, a, s, c):
                if a is not None:
                    add_xa(a, 0)
                    add_xa(a, 1)
                if s is not None:
                    outer(s, 1)
                if c is not None:
                    pool.wait_ge(o_in.sem, o_in.at(c, 2))
                    alone(pool)
                    nc.gpsimd.tensor_tensor(o[:, :, :], o[:, :, :], bv[:, :, :], ALU.add).then_inc(o_made.sem, 1)
                if a is not None:
                    add_xa(a, 2)
                if s is not None:
                    outer(s, 2)
                if a is not None:
                    add_xa(a, 3)
                if c is not None:
                    pool.wait_ge(rstd_made.sem, rstd_made.at(c, 1))
                    alone(pool)
                    nc.gpsimd.tensor_tensor(o[:, :, :], o[:, :, :], sq[:, :, :], ALU.mult).then_inc(y_made.sem, 1)
                if s is not None:
                    outer(s, 3)
                if a is not None:
                    add_xa(a, 4)
                if s is not None:
                    outer(s, 4)
                if n is not None:
                    pool.wait_ge(*emptied(n, "xaT", 1))
                    alone(pool)
                    nc.gpsimd.tensor_tensor(sx[:, :, :], xaT[:, :, 0:SEQ], xaT[:, :, 1:SEQ + 1], ALU.subtract)\
                        .then_inc(sx_made.sem, 1)
                if s is not None:
                    outer(s, 5)
                if c is not None:
                    pool.wait_ge(*emptied(c, "xcT", 1))
                    alone(pool)
                    nc.gpsimd.tensor_tensor(sx2[:, :, :], xcT[:, :, 0:SEQ], xcT[:, :, 1:SEQ + 1], ALU.subtract)\
                        .then_inc(sx2_made.sem, 1)
                if s is not None:
                    outer(s, 6)
                    outer(s, 7)
                if a is not None:
                    outer(a, 0)

            kv_made.prime(pool)
            pipeline(pool, body)

        @block.tensor
        def _(pe):
            pe.wait_ge(vectors_in, 16 * N_FIRST_DMAS)
            pe.wait_ge(consts_made, 3)
            for c in range(CG):
                last = nc.tensor.transpose(BANKS["n"][0][:, c * 2 * BATCH:(c + 1) * 2 * BATCH],
                                           state_rows[:, c * P:(c + 1) * P], ident[0:2 * BATCH, 0:2 * BATCH])
            last.then_inc(state_turned, 1)
            pe.wait_ge(state_kept, 1)

            def turn(b, name, src):
                for k in range(2):
                    pe.wait_ge(*bank_free(b, name, k))
                    for m in range(2):
                        for a in range(TT):
                            c = 2 * k + m
                            last = nc.tensor.transpose(tile(name, k)[:, m * SEQ + a * P:m * SEQ + (a + 1) * P],
                                                       src[:, a, c * P:(c + 1) * P], ident[:, :])
                    last.then_inc(full_sem(name), 1)

            def project_T(b, name, w, act):
                for k in range(2):
                    pe.wait_ge(*bank_free(b, name, k))
                    for m in range(2):
                        for c in range(CG):
                            last = nc.tensor.matmul(tile(name, k)[:, m * SEQ:(m + 1) * SEQ],
                                                    w[:, c, (2 * k + m) * P:(2 * k + m + 1) * P], act[:, c, :],
                                                    start=(c == 0), stop=(c == CG - 1))
                    last.then_inc(full_sem(name), 1)

            def project(b, name, w, act):
                for a in range(TT):
                    pe.wait_ge(*bank_free(b, name, a))
                    for c in range(CG):
                        last = nc.tensor.matmul(tile(name, a)[:, :], act[:, c, a * P:(a + 1) * P], w[:, c, :],
                                                start=(c == 0), stop=(c == CG - 1))
                    last.then_inc(full_sem(name), 1)

            def by_group(b, name, weight_of, act_of):
                for k in range(2):
                    pe.wait_ge(*bank_free(b, name, k))
                    for m in range(2):
                        last = nc.tensor.matmul(tile(name, k)[:, m * SEQ:(m + 1) * SEQ], weight_of(2 * k + m),
                                                act_of(2 * k + m), start=True, stop=True)
                    last.then_inc(full_sem(name), 1)

            def mix(a, f):
                if f < MIX - 1:
                    pe.wait_ge(f_made.sem, f_made.at(a, f + 1))
                by_group(a, f"mix{f}", lambda c: maa_w2[:, f // 4, c * P:(c + 1) * P],
                         lambda c: t1f[:, f % 2, :] if f < MIX - 1 else t1[:, 1, :])

            def body(n, a, s, c):
                if a is not None:
                    mix(a, 0)
                    mix(a, 1)
                    pe.wait_ge(mix_made.sem, mix_made.at(a, 1))
                    project_T(a, "k", W["Wk"], mixed[:, 0, :, :])
                if c is not None:
                    pe.wait_ge(o_made.sem, o_made.at(c, 1))
                    by_group(c, "mean", lambda cg: mean_head[:, :], lambda cg: o[:, cg, :])
                if a is not None:
                    mix(a, 2)
                    pe.wait_ge(mix_made.sem, mix_made.at(a, 2))
                    pe.wait_ge(*bank_free(a, "td1", 0))
                    for cg in range(CG):
                        last = nc.tensor.matmul(tile("td1", 0)[:, 0:SEQ], td_w1[:, cg, :], mixed[:, 1, cg, :],
                                                start=(cg == 0), stop=(cg == CG - 1))
                    last.then_inc(full["a"].sem, 1)
                if c is not None:
                    pe.wait_ge(sq_made.sem, sq_made.at(c, 1))
                    by_group(c, "var", lambda cg: mean_head[:, :], lambda cg: sq[:, cg, :])
                if a is not None:
                    mix(a, 3)
                    pe.wait_ge(*emptied(a, "td1", 0))
                    by_group(a, "td2", lambda cg: td_w2[:, cg * P:(cg + 1) * P], lambda cg: tdt[:, :])
                    pe.wait_ge(mix_made.sem, mix_made.at(a, 3))
                    project_T(a, "v", W["Wv"], mixed[:, 0, :, :])
                    mix(a, 4)
                    pe.wait_ge(mix_made.sem, mix_made.at(a, 4))
                    project_T(a, "r", W["Wr"], mixed[:, 1, :, :])
                if c is not None:
                    pe.wait_ge(yg_made.sem, yg_made.at(c, 1))
                    project(c, "wo", W["Wo"], o)
                if a is not None:
                    pe.wait_ge(mix_made.sem, mix_made.at(a, 5))
                    project_T(a, "g", W["Wg"], mixed[:, 0, :, :])
                if n is not None:
                    pe.wait_ge(a_h.sem, a_h.at(n, 1))
                    turn(n, "xaT", xa)
                if c is not None:
                    pe.wait_ge(c_h.sem, c_h.at(c, 1))
                    turn(c, "xcT", sq[:, :, :].rearrange("p c t -> p (c t)").rearrange("p (a n) -> p a n", a=TT))
                if a is not None:
                    pe.wait_ge(rku_made.sem, rku_made.at(a, 2))
                    by_group(a, "bonus", lambda cg: same_head[:, :], lambda cg: mixed[:, 1, cg, :])
                if n is not None:
                    pe.wait_ge(z_made.sem, z_made.at(n, 1))
                    pe.wait_ge(*bank_free(n, "t1", 0))
                    for m in range(2):
                        for cg in range(CG):
                            last = nc.tensor.matmul(tile("t1", 0)[:, m * SEQ:(m + 1) * SEQ],
                                                    maa_w1[:, cg, m * P:(m + 1) * P], z[:, cg, :],
                                                    start=(cg == 0), stop=(cg == CG - 1))
                    last.then_inc(full["n"].sem, 1)
                if c is not None:
                    pe.wait_ge(xr_made.sem, xr_made.at(c, 1))
                    project(c, "rr", W["Wfr"], g)
                    project_T(c, "kk", W["Wfk"], bv)
                    pe.wait_ge(kk_made.sem, kk_made.at(c, 1))
                    project(c, "kv", W["Wfv"], sq)

            for tally in full.values():
                tally.prime(pe)
            pipeline(pe, body, lambda: pe.wait_ge(weights_in, 16 * N_WEIGHT_DMAS))

        @block.vector
        def _(dve):
            dve.wait_ge(vectors_in, 16 * N_FIRST_DMAS)
            dve.wait_ge(consts_made, 3)
            dve.wait_ge(state_turned, 1)
            nc.vector.tensor_copy(stateT[:, :, :].rearrange("p c b -> p (c b)"),
                                  BANKS["n"][0][:, 0:CG * 2 * BATCH]).then_inc(state_kept, 1)

            def layernorm(b, i, src, dst, links, var_made, std_made, h_made):
                for a in range(TT):
                    nc.vector.bn_stats(stats[:, i, a, :], src[:, a, :]).then_inc(links.sem, 1)
                dve.wait_ge(links.sem, links.at(b, TT))
                alone(dve)
                for a in range(TT):
                    last = nc.vector.bn_aggr(meanvar[:, i, a, :], stats[:, i, a, :])
                last.then_inc(var_made.sem, 1)
                dve.wait_ge(std_made.sem, std_made.at(b, 1))
                nc.vector.reciprocal(rstd[:, i, :], std[:, i, :]).then_inc(links.sem, 1)
                dve.wait_ge(links.sem, links.at(b, TT + 1))
                for a in range(TT):
                    last = nc.vector.tensor_scalar(dst[:, a, :], src[:, a, :], meanvar[:, i, a, 0:1], rstd[:, i, a:a + 1],
                                                   ALU.subtract, ALU.mult)
                last.then_inc(h_made.sem, 1)

            def step(s, u):
                q, jp = u // JP, u % JP
                slot = ring[:, u % 2, :, :, :]
                dve.wait_ge(kv_made.sem, kv_made.at(s, u + 1))
                if jp == 0:
                    dve.wait_ge(wkr_in[q % 2].sem, wkr_in[q % 2].at(s, q // 2 + 1))
                alone(dve)
                decay = flat(ws[:, q % 2, :, :])
                for j in range(JCOLS):
                    x_ = flat(slot[:, j, :, :])
                    last = nc.vector.tensor_tensor_scan(x_, decay, x_, 0.0, ALU.mult, ALU.add)
                last.then_inc(scanned.sem, 1)
                dve.wait_ge(scanned.sem, scanned.at(s, u + 1))
                x_ = slot[:, :, :, 0:SEQ]
                nc.vector.tensor_tensor(x_, x_, rs[:, q % 2, :, :].unsqueeze(1).to_broadcast([P, JCOLS, IROWS, SEQ]),
                                        ALU.mult).then_inc(weighed.sem, 1)
                dve.wait_ge(weighed.sem, weighed.at(s, u + 1))
                if u == 0:
                    dve.wait_ge(o_out.sem, o_out.at(s, 0))
                dst = osum[:, jp * JCOLS:(jp + 1) * JCOLS, :]
                to = dst if q == 0 else part[:, :, :]
                nc.vector.tensor_reduce(to, x_.rearrange("p j i t -> p j t i"), AX_X, ALU.add).then_inc(reduced.sem, 1)
                if q:
                    dve.wait_ge(reduced.sem, reduced.at(s, u + 1))
                    nc.vector.tensor_tensor(dst, dst, part[:, :, :], ALU.add).then_inc(summed.sem, 1)

            def shift(a, f):
                for k in range(2):
                    dve.wait_ge(*filled(a, f"mix{f}", k))
                    if f == 0 and k == 0:
                        dve.wait_ge(bv_out.sem, bv_out.at(a, 0))
                    for m in range(2):
                        c = 2 * k + m
                        last = nc.vector.scalar_tensor_tensor(out=mixed[:, f % 2, c, :],
                                                              in0=tile(f"mix{f}", k)[:, m * SEQ:(m + 1) * SEQ],
                                                              scalar=col(f"stack{f}", c), in1=sx[:, c, :],
                                                              op0=ALU.add, op1=ALU.mult)
                    last.then_inc(empty_sem(f"mix{f}"), 1)

            def body(n, a, s, c):
                if a is not None:
                    shift(a, 0)
                    nc.vector.tensor_scalar(t1f[:, 0, :], t1[:, 0, :], f_row[:, 2:3], None, ALU.mult)\
                        .then_inc(f_made.sem, 1)
                    shift(a, 1)
                    nc.vector.tensor_scalar(t1f[:, 1, :], t1[:, 0, :], f_row[:, 3:4], None, ALU.mult)\
                        .then_inc(f_made.sem, 1)
                if s is not None:
                    step(s, 0)
                if a is not None:
                    shift(a, 2)
                if c is not None:
                    for k in range(2):
                        dve.wait_ge(*filled(c, "mean", k))
                        x_ = flat(o[:, 2 * k:2 * k + 2, :])
                        nc.vector.tensor_tensor(x_, x_, tile("mean", k)[:, :], ALU.subtract)\
                            .then_inc(empty_sem("mean"), 1)
                if s is not None:
                    step(s, 1)
                if a is not None:
                    shift(a, 3)
                if c is not None:
                    dve.wait_ge(*emptied(c, "var", 1))
                    nc.vector.reciprocal(sq[:, :, :], sq[:, :, :]).then_inc(rstd_made.sem, 1)
                if s is not None:
                    step(s, 2)
                if a is not None:
                    shift(a, 4)
                if c is not None:
                    dve.wait_ge(yn_made.sem, yn_made.at(c, 1))
                    dve.wait_ge(c_in.sem, c_in.at(c, 2))
                    nc.vector.scalar_tensor_tensor(out=flat(o[:, :, :]), in0=flat(o[:, :, :]), scalar=0.5,
                                                   in1=flat(g[:, :, :]), op0=ALU.mult, op1=ALU.mult)\
                        .then_inc(yg_made.sem, 1)
                if s is not None:
                    step(s, 3)
                if n is not None:
                    dve.wait_ge(xa_in.sem, xa_in.at(n, 1))
                    layernorm(n, 0, xa, xa, a_links, a_var, a_std, a_h)
                if a is not None:
                    dve.wait_ge(*emptied(a, "r", 1))
                    for cg in range(CG):
                        last = nc.vector.scalar_tensor_tensor(out=mixed[:, 1, cg, :], in0=kT[:, cg, :],
                                                              scalar=col("u_flat", cg), in1=rT[:, cg, :],
                                                              op0=ALU.mult, op1=ALU.mult)
                        if cg % 2:
                            last.then_inc(rku_made.sem, 1)
                if c is not None:
                    for k in range(TT):
                        dve.wait_ge(*filled(c, "wo", k))
                        nc.vector.tensor_tensor(xr[:, k, :], tile("wo", k)[:, :], xr[:, k, :], ALU.add)\
                            .then_inc(empty_sem("wo"), 1)
                    dve.wait_ge(*emptied(c, "wo", 1))
                    h2 = flat(sq[:, :, :]).rearrange("p (a n) -> p a n", a=TT)
                    layernorm(c, 1, xr, h2, c_links, c_var, c_std, c_h)
                if s is not None:
                    step(s, 4)
                if a is not None:
                    for k in range(2):
                        dve.wait_ge(tanh_g.sem, tanh_g.at(a, k + 1))
                        x_ = flat(gT[:, 2 * k:2 * k + 2, :])
                        nc.vector.scalar_tensor_tensor(out=x_, in0=x_, scalar=1.0, in1=tile("g", k)[:, :],
                                                       op0=ALU.add, op1=ALU.mult).then_inc(empty_sem("g"), 1)
                if n is not None:
                    dve.wait_ge(sx_made.sem, sx_made.at(n, 1))
                    for cg in range(CG):
                        last = nc.vector.scalar_tensor_tensor(out=z[:, cg, :], in0=sx[:, cg, :],
                                                              scalar=col("maa_x", cg), in1=xaT[:, cg, 1:SEQ + 1],
                                                              op0=ALU.mult, op1=ALU.add)
                    last.then_inc(z_made.sem, 1)
                if c is not None:
                    dve.wait_ge(sx2_made.sem, sx2_made.at(c, 1))
                    for dst, name in ((g, "ffn_maa_r"), (bv, "ffn_maa_k")):
                        for cg in range(CG):
                            last = nc.vector.scalar_tensor_tensor(out=dst[:, cg, :], in0=sx2[:, cg, :],
                                                                  scalar=col(name, cg), in1=xcT[:, cg, 1:SEQ + 1],
                                                                  op0=ALU.mult, op1=ALU.add)
                    last.then_inc(xr_made.sem, 1)
                if s is not None:
                    step(s, 5)
                if a is not None:
                    for k in range(2):
                        dve.wait_ge(*filled(a, "bonus", k))
                        nc.vector.tensor_tensor(flat(mixed[:, 0, 2 * k:2 * k + 2, :]), tile("bonus", k)[:, :],
                                                flat(vT[:, 2 * k:2 * k + 2, :]), ALU.mult)\
                            .then_inc(empty_sem("bonus"), 1)
                if n is not None:
                    dve.wait_ge(*emptied(n, "t1", 0))
                    for f in range(2):
                        nc.vector.tensor_scalar(t1f[:, f, :], t1[:, 0, :], f_row[:, f:f + 1], None, ALU.mult)\
                            .then_inc(f_made.sem, 1)
                if s is not None:
                    step(s, 6)
                if s is not None:
                    step(s, 7)
                if c is not None:
                    dve.wait_ge(*emptied(c, "rr", 1))
                    nc.vector.tensor_scalar(o[:, :, :], o[:, :, :], 0.5, 0.5, ALU.mult, ALU.add).then_inc(rr_made.sem, 1)
                    dve.wait_ge(rr_made.sem, rr_made.at(c, 1))
                    for k in range(TT):
                        dve.wait_ge(*filled(c, "kv", k))
                        x_ = flat(o[:, 2 * k:2 * k + 2, :])
                        nc.vector.tensor_tensor(x_, x_, tile("kv", k)[:, :], ALU.mult).then_inc(empty_sem("kv"), 1)
                    dve.wait_ge(*emptied(c, "kv", 1))
                    nc.vector.tensor_tensor(xr[:, :, :].rearrange("p a n -> p (a n)"),
                                            xr[:, :, :].rearrange("p a n -> p (a n)"), flat(o[:, :, :]), ALU.add)\
                        .then_inc(out_made.sem, 1)

            for tally in (taken["a"]["dve"], taken["c"]["dve"], weighed, reduced):
                tally.prime(dve)
            pipeline(dve, body)

        @block.scalar
        def _(act):
            act.wait_ge(vectors_in, 16 * N_FIRST_DMAS)
            act.wait_ge(consts_made, 3)
            act.wait_ge(state_kept, 1)

            def root(b, i, var_made, std_made):
                act.wait_ge(var_made.sem, var_made.at(b, 1))
                nc.scalar.activation(std[:, i, :], meanvar[:, i, :, 1], ACT.Sqrt, bias=eps_col[:, :])\
                    .then_inc(std_made.sem, 1)

            def take_ln(b, name, dst, scale, bias, which):
                nc.scalar.copy(dst[:, :, 0:1], stateT[:, :, bass.ds(2 * b + which, 1)])
                for k in range(2):
                    act.wait_ge(*filled(b, name, k))
                    for m in range(2):
                        cg = 2 * k + m
                        last = nc.scalar.activation(dst[:, cg, 1:SEQ + 1], tile(name, k)[:, m * SEQ:(m + 1) * SEQ],
                                                    ACT.Identity, bias=col(bias, cg), scale=col(scale, cg))
                    last.then_inc(empty_sem(name), 1)

            def take(a, name, dst, dram_):
                for k in range(2):
                    act.wait_ge(*filled(a, name, k))
                    if k == 0:
                        act.wait_ge(kwvr_out.sem, kwvr_out.at(a, 0))
                    nc.scalar.activation(flat(dst[:, 2 * k:2 * k + 2, :]), tile(name, k)[:, :], ACT.Copy).then_inc(empty_sem(name), 1)
                act.wait_ge(*emptied(a, name, 1))
                alone(act)
                act.dma_start(dram_[a, :, :].rearrange("(c p) t -> p c t", p=P), dst[:, :, :])\
                    .then_inc(kwvr_out.sem, 16)

            def body(n, a, s, c):
                if a is not None:
                    take(a, "k", kT, k_dram)
                if c is not None:
                    act.wait_ge(*emptied(c, "mean", 1))
                    nc.scalar.activation(sq[:, :, :], o[:, :, :], ACT.Square).then_inc(sq_made.sem, 1)
                if a is not None:
                    act.wait_ge(*filled(a, "td1", 0))
                    nc.scalar.activation(tdt[:, :], tile("td1", 0)[:, 0:SEQ], ACT.Tanh).then_inc(empty_sem("td1"), 1)
                if c is not None:
                    act.wait_ge(*filled(c, "var", 1))
                    for k in range(2):
                        nc.scalar.activation(flat(sq[:, 2 * k:2 * k + 2, :]), tile("var", k)[:, :], ACT.Sqrt,
                                             bias=eps_col[:, :]).then_inc(empty_sem("var"), 1)
                if a is not None:
                    for k in range(2):
                        act.wait_ge(*filled(a, "td2", k))
                        if k == 0:
                            act.wait_ge(kwvr_out.sem, kwvr_out.at(a, 0))
                        for m in range(2):
                            cg = 2 * k + m
                            last = nc.scalar.activation(wT[:, cg, 1:SEQ + 1], tile("td2", k)[:, m * SEQ:(m + 1) * SEQ],
                                                        ACT.Exp, bias=col("time_decay", cg))
                        last.then_inc(empty_sem("td2"), 1)
                    act.wait_ge(*emptied(a, "td2", 1))
                    nc.scalar.activation(wT[:, :, 1:SEQ + 1], wT[:, :, 1:SEQ + 1], ACT.Exp, scale=-1.0)\
                        .then_inc(w_made.sem, 1)
                    act.wait_ge(w_made.sem, w_made.at(a, 1))
                    alone(act)
                    act.dma_start(w_dram[a, :, :].rearrange("(c p) t -> p c t", p=P), wT[:, :, :])\
                        .then_inc(kwvr_out.sem, 16)
                    take(a, "v", vT, v_dram)
                if c is not None:
                    act.wait_ge(y_made.sem, y_made.at(c, 1))
                    for cg in range(CG):
                        last = nc.scalar.activation(o[:, cg, :], o[:, cg, :], ACT.Identity, bias=col("gn_b", cg),
                                                    scale=col("gn_w", cg))
                    last.then_inc(yn_made.sem, 1)
                if a is not None:
                    take(a, "r", rT, r_dram)
                if n is not None:
                    root(n, 0, a_var, a_std)
                if c is not None:
                    root(c, 1, c_var, c_std)
                if a is not None:
                    for k in range(2):
                        act.wait_ge(*filled(a, "g", k))
                        if k == 0:
                            act.wait_ge(g_out.sem, g_out.at(a, 0))
                        nc.scalar.activation(flat(gT[:, 2 * k:2 * k + 2, :]), tile("g", k)[:, :], ACT.Tanh, scale=0.5)\
                            .then_inc(tanh_g.sem, 1)
                if n is not None:
                    take_ln(n, "xaT", xaT, "m_ln1_w", "m_ln1_b", 1)
                if c is not None:
                    take_ln(c, "xcT", xcT, "m_ln2_w", "m_ln2_b", 0)
                if n is not None:
                    act.wait_ge(*filled(n, "t1", 0))
                    nc.scalar.activation(t1[:, :, :], tile("t1", 0)[:, :].rearrange("p (m t) -> p m t", m=2), ACT.Tanh)\
                        .then_inc(empty_sem("t1"), 1)
                if c is not None:
                    for k in range(TT):
                        act.wait_ge(*filled(c, "rr", k))
                        nc.scalar.activation(flat(o[:, 2 * k:2 * k + 2, :]), tile("rr", k)[:, :], ACT.Tanh, scale=0.5)\
                            .then_inc(empty_sem("rr"), 1)
                    for k in range(2):
                        act.wait_ge(*filled(c, "kk", k))
                        nc.scalar.activation(flat(sq[:, 2 * k:2 * k + 2, :]), tile("kk", k)[:, :], ACT.Relu)\
                            .then_inc(empty_sem("kk"), 1)
                    act.wait_ge(*emptied(c, "kk", 1))
                    nc.scalar.activation(sq[:, :, :], sq[:, :, :], ACT.Square).then_inc(kk_made.sem, 1)

            for tally in (taken["n"]["act"], taken["a"]["act"], taken["c"]["act"], kwvr_out):
                tally.prime(act)
            pipeline(act, body)


def two_layers(nc, T, out_dram):
    vectors(T)
    vectors_b(T)
    with ExitStack() as sems:
        x3_dram = nc.dram_tensor("x3_all", [BATCH, SEQ, DM], F32, kind="Internal").ap()
        attention_block(nc, sems, T, x3_dram)
        recurrent_block(nc, sems, T, x3_dram, out_dram)


_INPUTS = {"x": "x", "enc": "ctx_2048", "mask_self": "mask_1x1xSxS2_fc1", "mask_cross": "mask_Bx1xSxS2_ff1",
           "m_ln1_w": "L1_xattn_ln1_w", "m_ln1_b": "L1_xattn_ln1_b", "m_ln2_w": "L1_xattn_ln2_w",
           "m_ln2_b": "L1_xattn_ln2_b"}
_INPUTS |= {n: "L0_xattn_" + n for n in ("ln1_s", "ln1_b", "w_qkv", "b_qkv", "w_ao", "b_ao", "ln2_s", "ln2_b", "w_q",
                                         "b_q", "w_kv", "b_kv", "w_co", "b_co", "ln3_s", "ln3_b", "w1", "b1", "w2",
                                         "b2")}
_INPUTS |= {n: "L1_xattn_" + n for n in ("maa_x", "maa_w1", "maa_w2", "maa_stack", "time_decay", "td_w1", "td_w2", "u",
                                         "Wr", "Wk", "Wv", "Wg", "Wo", "gn_w", "gn_b", "ffn_maa_k", "ffn_maa_r", "Wfk",
                                         "Wfr", "Wfv")}
_TURNED = ("Wr", "Wk", "Wv", "Wg", "Wo", "Wfk", "Wfr", "Wfv")


def kernel(**inputs):
    import numpy as np
    import concourse.bacc as bacc
    from concourse.bass_utils import run_bass_kernel_spmd as run

    nc = bacc.Bacc("TRN2", target_bir_lowering=False, num_devices=1)
    arrays, T = {}, {}
    for name, given in _INPUTS.items():
        a = np.asarray(inputs[given])
        a = np.ascontiguousarray(a.T if name in _TURNED else a)
        arrays[f"in_{name}_dram"] = a
        T[name] = nc.dram_tensor(f"in_{name}_dram", a.shape, mybir.dt.from_np(a.dtype), kind="ExternalInput").ap()
    T["mask_self"] = T["mask_self"][0, 0, :, :]
    T["mask_cross"] = T["mask_cross"][:, 0, :, :]
    out = nc.dram_tensor("out_0_dram", (BATCH, SEQ, DM), F32, kind="ExternalOutput").ap()
    two_layers(nc, T, out)
    r = run(nc, [arrays], core_ids=[0])
    return r.results[0]["out_0_dram"]
```
